# Optimizing a Trainium2 kernel written in Bass

```python
import numpy as np
import jax
import jax.numpy as jnp

def _softmax(x, axis=-1):
    return jax.nn.softmax(x, axis=axis)

def _gelu(x):
    return jax.nn.gelu(x, approximate=True)

def _silu(x):
    return jax.nn.silu(x)

def _sigmoid(x):
    return jax.nn.sigmoid(x)

def _layernorm(x, axis=-1, eps=1e-05):
    m = jnp.mean(x, axis=axis, keepdims=True)
    v = jnp.var(x, axis=axis, keepdims=True)
    return (x - m) / jnp.sqrt(v + eps)

def _scatter_add(tgt, idx, src, axis=0):
    return tgt.at[idx].add(src)

def _segment_sum(src, seg, n):
    return jax.ops.segment_sum(src, seg, n)
kernel_name = 'mk_flamingo_gated_d2_seqx_r8_c12555'

def setup_inputs(seed: int=0):
    np.random.seed(seed)
    _w = jnp.asarray

    def _rec_inputs():
        import jax
        import jax.numpy as jnp
        _rk = jax.random.key(seed)
        x = 7.22e-05 + 1 * jax.random.normal(jax.random.fold_in(_rk, 1), (8, 128, 512), jnp.float32)
        _lenS = 128 - jax.random.randint(jax.random.fold_in(_rk, 7), (8,), 0, max(1, 128 // 4) + 1, jnp.int32)
        _lenS2 = 128 - jax.random.randint(jax.random.fold_in(_rk, 8), (8,), 0, max(1, 128 // 4) + 1, jnp.int32)
        _ctx_4096P = jax.random.normal(jax.random.fold_in(_rk, 11), (8, 16, 512), jnp.float32)
        _ctx_4096c = jax.random.dirichlet(jax.random.fold_in(_rk, 511), 0.3 * jnp.ones((16,), jnp.float32), (8, 128))
        _ctx_4096t = jnp.einsum('bsk,bkd->bsd', _ctx_4096c, _ctx_4096P)
        _ctx_4096t = _ctx_4096t * jax.lax.rsqrt(jnp.mean(jnp.square(_ctx_4096t)) + 1e-12) * 0.953939
        ctx_4096 = 4.13588e-05 + 0.999923 * (_ctx_4096t + 0.3 * jax.random.normal(jax.random.fold_in(_rk, 611), (8, 128, 512), jnp.float32))
        _validS = jnp.arange(128)[None, :] < _lenS[:, None]
        _validS2 = jnp.arange(128)[None, :] < _lenS2[:, None]
        _causal = jnp.tril(jnp.ones((128, 128), dtype=bool))
        mask_1x1xSxS2_bk0 = jnp.logical_not(jnp.broadcast_to(_validS2[0:1, None, None, :], (1, 1, 128, 128)))
        mask_Bx1x4096_ff1 = jnp.where(jnp.ones((8, 1, 512), dtype=bool), 1.0, 0.0).astype(jnp.float32)
        _g = jax.random.normal(jax.random.fold_in(_rk, 9001), (2, 2), jnp.float32)
        _g = jnp.sign(_g) * jnp.maximum(jnp.abs(_g), 1.0) + (_g == 0) * 1.0
        g_xattn = _g[0]
        g_ffn = _g[1]
        return (x, ctx_4096, mask_1x1xSxS2_bk0, mask_Bx1x4096_ff1, g_xattn, g_ffn)
    x, ctx_4096, mask_1x1xSxS2_bk0, mask_Bx1x4096_ff1, g_xattn, g_ffn = _rec_inputs()

    def _L0_xattn_setup():
        import jax, jax.numpy as jnp
        import numpy as np
        B, T, D_MODEL = (1, 256, 512)
        NUM_Q_HEADS, NUM_KV_HEADS, KEY_SIZE = (32, 8, 128)
        ATTN_MULT = 0.08838834764831845
        MAX_ATTN_VAL = 30.0

        def rotate_half(x):
            x1, x2 = jnp.split(x, 2, axis=-1)
            return jnp.concatenate((-x2, x1), axis=-1)

        def apply_rope(x):
            b, t, h, d = x.shape
            exponents = jnp.arange(0, d, 2, dtype=jnp.float32)
            inv_freq = 1.0 / 10000.0 ** (exponents / d)
            pos = jnp.arange(t, dtype=jnp.float32)
            phase = pos[:, None] * inv_freq[None, :]
            phase = jnp.tile(phase, (1, 2))[None, :, None, :]
            return (x * jnp.cos(phase) + rotate_half(x) * jnp.sin(phase)).astype(x.dtype)
        key = jax.random.key(seed)
        ks = jax.random.split(key, 8)
        query = jax.random.normal(ks[0], (B, T, D_MODEL), dtype=jnp.float32)
        kk = jax.random.normal(ks[1], (B, T, D_MODEL), dtype=jnp.float32)
        vv = jax.random.normal(ks[2], (B, T, D_MODEL), dtype=jnp.float32)
        mask = jnp.tril(jnp.ones((T, T), dtype=bool))[None, None, :, :]
        s = 0.02
        Wq = jax.random.normal(ks[3], (D_MODEL, NUM_Q_HEADS * KEY_SIZE), dtype=jnp.float32) * s
        Wk = jax.random.normal(ks[4], (D_MODEL, NUM_KV_HEADS * KEY_SIZE), dtype=jnp.float32) * s
        Wv = jax.random.normal(ks[5], (D_MODEL, NUM_KV_HEADS * KEY_SIZE), dtype=jnp.float32) * s
        Wo = jax.random.normal(ks[6], (NUM_Q_HEADS * KEY_SIZE, D_MODEL), dtype=jnp.float32) * s
        return {'query': query, 'key': kk, 'value': vv, 'mask': mask, 'Wq': Wq, 'Wk': Wk, 'Wv': Wv, 'Wo': Wo}
    _L0_xattn_all = _L0_xattn_setup()
    _L0_xattn_in = {k: v for k, v in _L0_xattn_all.items() if k in ('Wq', 'Wk', 'Wv', 'Wo')}
    del _L0_xattn_all

    def _L0_ffn_setup():
        import jax, jax.numpy as jnp
        import numpy as np
        SCALING = 16.0 / 8.0
        GAMMA = 1.0
        EPS = 1e-12
        key = jax.random.key(seed)
        ks = jax.random.split(key, 8)
        B, T, H, O = (4, 256, 512, 512)
        E_tot, E_act, r = (16, 4, 8)
        return {'x': jax.random.normal(ks[0], (B, T, H), jnp.float32), 'W_base': jax.random.normal(ks[1], (O, H), jnp.float32) * 0.02, 'b_base': jax.random.normal(ks[2], (O,), jnp.float32) * 0.02, 'lora_A': jax.random.normal(ks[3], (E_tot, r, H), jnp.float32) * 0.02, 'lora_B': jax.random.normal(ks[4], (E_tot, O, r), jnp.float32) * 0.02, 'router_W': jax.random.normal(ks[5], (E_tot, H), jnp.float32) * 0.02, 'router_b': jax.random.normal(ks[6], (E_tot,), jnp.float32) * 0.02, 'domain_prior': jax.random.uniform(ks[7], (E_tot,), jnp.float32), 'active': jnp.arange(E_act, dtype=jnp.int32)}
    _L0_ffn_all = _L0_ffn_setup()
    _L0_ffn_in = {k: v for k, v in _L0_ffn_all.items() if k in ('W_base', 'b_base', 'lora_A', 'lora_B', 'router_W', 'router_b', 'domain_prior', 'active')}
    del _L0_ffn_all

    def _L1_xattn_setup():
        import jax, jax.numpy as jnp
        import numpy as np
        W = 128
        H = 8
        D = 128
        DK = D // 2

        def _to_patches(x):
            b, d, s = x.shape
            np_ = s // W
            return x.reshape(b, d, np_, W).transpose(0, 2, 1, 3).reshape(b * np_, d, W)
        key = jax.random.key(seed)
        ks = jax.random.split(key, 10)
        B, S = (8, 512)
        qk = jax.random.normal(ks[0], (B, D, S), dtype=jnp.float32)
        v = jax.random.normal(ks[1], (B, D, S), dtype=jnp.float32)
        masks = jnp.ones((B, 1, S), dtype=jnp.float32)
        sc = 1.0 / np.sqrt(D)
        Wq = jax.random.normal(ks[2], (DK, D), dtype=jnp.float32) * sc
        bq = jnp.zeros((DK,), dtype=jnp.float32)
        Wk = jax.random.normal(ks[3], (DK, D), dtype=jnp.float32) * sc
        bk = jnp.zeros((DK,), dtype=jnp.float32)
        Wv = jax.random.normal(ks[4], (DK, D), dtype=jnp.float32) * sc
        bv = jnp.zeros((DK,), dtype=jnp.float32)
        Wo = jax.random.normal(ks[5], (D, DK), dtype=jnp.float32) * (1.0 / np.sqrt(DK))
        bo = jnp.zeros((D,), dtype=jnp.float32)
        return dict(qk=qk, v=v, masks=masks, Wq=Wq, bq=bq, Wk=Wk, bk=bk, Wv=Wv, bv=bv, Wo=Wo, bo=bo)
    _L1_xattn_all = _L1_xattn_setup()
    _L1_xattn_in = {k: v for k, v in _L1_xattn_all.items() if k in ('Wq', 'bq', 'Wk', 'bk', 'Wv', 'bv', 'Wo', 'bo')}
    del _L1_xattn_all

    def _L1_ffn_setup():
        import jax, jax.numpy as jnp
        import numpy as np
        TOP_K = 2
        key = jax.random.key(seed)
        k0, k1, k2 = jax.random.split(key, 3)
        B, S, D, H, E = (4, 256, 512, 512, 8)
        sc = 1.0 / np.sqrt(D).astype(np.float32)
        x = jax.random.normal(k0, (B, S, D), dtype=jnp.float32)
        W_gate = jax.random.normal(k1, (D, E), dtype=jnp.float32) * sc
        b_gate = jnp.zeros((E,), dtype=jnp.float32)
        W_e = jax.random.normal(k2, (E, D, H), dtype=jnp.float32) * sc
        b_e = jnp.zeros((E, H), dtype=jnp.float32)
        return {'x': x, 'W_gate': W_gate, 'b_gate': b_gate, 'W_e': W_e, 'b_e': b_e}
    _L1_ffn_all = _L1_ffn_setup()
    _L1_ffn_in = {k: v for k, v in _L1_ffn_all.items() if k in ('W_gate', 'b_gate', 'W_e', 'b_e')}
    del _L1_ffn_all
    return {'x': x, 'ctx_4096': ctx_4096, 'mask_1x1xSxS2_bk0': mask_1x1xSxS2_bk0, 'mask_Bx1x4096_ff1': mask_Bx1x4096_ff1, 'g_xattn': g_xattn, 'g_ffn': g_ffn, 'L0_xattn_Wq': _L0_xattn_in['Wq'], 'L0_xattn_Wk': _L0_xattn_in['Wk'], 'L0_xattn_Wv': _L0_xattn_in['Wv'], 'L0_xattn_Wo': _L0_xattn_in['Wo'], 'L0_ffn_W_base': _L0_ffn_in['W_base'], 'L0_ffn_b_base': _L0_ffn_in['b_base'], 'L0_ffn_lora_A': _L0_ffn_in['lora_A'], 'L0_ffn_lora_B': _L0_ffn_in['lora_B'], 'L0_ffn_router_W': _L0_ffn_in['router_W'], 'L0_ffn_router_b': _L0_ffn_in['router_b'], 'L0_ffn_domain_prior': _L0_ffn_in['domain_prior'], 'L0_ffn_active': _L0_ffn_in['active'], 'L1_xattn_Wq': _L1_xattn_in['Wq'], 'L1_xattn_bq': _L1_xattn_in['bq'], 'L1_xattn_Wk': _L1_xattn_in['Wk'], 'L1_xattn_bk': _L1_xattn_in['bk'], 'L1_xattn_Wv': _L1_xattn_in['Wv'], 'L1_xattn_bv': _L1_xattn_in['bv'], 'L1_xattn_Wo': _L1_xattn_in['Wo'], 'L1_xattn_bo': _L1_xattn_in['bo'], 'L1_ffn_W_gate': _L1_ffn_in['W_gate'], 'L1_ffn_b_gate': _L1_ffn_in['b_gate'], 'L1_ffn_W_e': _L1_ffn_in['W_e'], 'L1_ffn_b_e': _L1_ffn_in['b_e']}

def reference(x, ctx_4096, mask_1x1xSxS2_bk0, mask_Bx1x4096_ff1, g_xattn, g_ffn, L0_xattn_Wq, L0_xattn_Wk, L0_xattn_Wv, L0_xattn_Wo, L0_ffn_W_base, L0_ffn_b_base, L0_ffn_lora_A, L0_ffn_lora_B, L0_ffn_router_W, L0_ffn_router_b, L0_ffn_domain_prior, L0_ffn_active, L1_xattn_Wq, L1_xattn_bq, L1_xattn_Wk, L1_xattn_bk, L1_xattn_Wv, L1_xattn_bv, L1_xattn_Wo, L1_xattn_bo, L1_ffn_W_gate, L1_ffn_b_gate, L1_ffn_W_e, L1_ffn_b_e):
    import jax
    import jax.numpy as jnp

    def _L0_xattn_ref(query, key, value, mask, Wq, Wk, Wv, Wo):
        import jax, jax.numpy as jnp
        import numpy as np
        B, T, D_MODEL = (1, 256, 512)
        NUM_Q_HEADS, NUM_KV_HEADS, KEY_SIZE = (32, 8, 128)
        ATTN_MULT = 0.08838834764831845
        MAX_ATTN_VAL = 30.0

        def rotate_half(x):
            x1, x2 = jnp.split(x, 2, axis=-1)
            return jnp.concatenate((-x2, x1), axis=-1)

        def apply_rope(x):
            b, t, h, d = x.shape
            exponents = jnp.arange(0, d, 2, dtype=jnp.float32)
            inv_freq = 1.0 / 10000.0 ** (exponents / d)
            pos = jnp.arange(t, dtype=jnp.float32)
            phase = pos[:, None] * inv_freq[None, :]
            phase = jnp.tile(phase, (1, 2))[None, :, None, :]
            return (x * jnp.cos(phase) + rotate_half(x) * jnp.sin(phase)).astype(x.dtype)
        b, t, _ = query.shape
        d = KEY_SIZE
        h, kv_h = (NUM_Q_HEADS, NUM_KV_HEADS)
        g = h // kv_h
        q = (query @ Wq).reshape(b, t, h, d)
        k = (key @ Wk).reshape(b, t, kv_h, d)
        v = (value @ Wv).reshape(b, t, kv_h, d)
        q = apply_rope(q)
        k = apply_rope(k)
        q = q.reshape(b, t, kv_h, g, d)
        logits = jnp.einsum('btkgd,bTkd->bkgtT', q, k).astype(jnp.float32)
        logits = logits * ATTN_MULT
        logits = MAX_ATTN_VAL * jnp.tanh(logits / MAX_ATTN_VAL)
        m = mask[:, :, None, :, :]
        logits = jnp.where(m, logits, -1e+30)
        weights = jax.nn.softmax(logits, axis=-1).astype(query.dtype)
        attn = jnp.einsum('bkgtT,bTkd->btkgd', weights, v)
        attn = attn.reshape(b, t, h * d)
        return attn @ Wo

    def _L0_ffn_ref(x, W_base, b_base, lora_A, lora_B, router_W, router_b, domain_prior, active):
        import jax, jax.numpy as jnp
        import numpy as np
        SCALING = 16.0 / 8.0
        GAMMA = 1.0
        EPS = 1e-12
        y = jnp.einsum('bth,oh->bto', x, W_base) + b_base
        A = lora_A[active]
        Bm = lora_B[active]
        z = jnp.einsum('bth,erh->bter', x, A)
        contribs = jnp.einsum('bter,eor->bteo', z, Bm) * SCALING
        logits = jnp.einsum('bth,eh->bte', x, router_W) + router_b
        logits = logits[..., active]
        prior = domain_prior[active]
        alpha = jax.nn.softmax(jnp.log(prior + EPS) + logits / GAMMA, axis=-1)
        return y + jnp.einsum('bteo,bte->bto', contribs, alpha)

    def _L1_xattn_ref(qk, v, masks, Wq, bq, Wk, bk, Wv, bv, Wo, bo):
        import jax, jax.numpy as jnp
        import numpy as np
        W = 128
        H = 8
        D = 128
        DK = D // 2

        def _to_patches(x):
            b, d, s = x.shape
            np_ = s // W
            return x.reshape(b, d, np_, W).transpose(0, 2, 1, 3).reshape(b * np_, d, W)
        B, _, S = qk.shape
        np_ = S // W
        qp = _to_patches(qk)
        vp = _to_patches(v)
        mp = _to_patches(masks)
        q = jnp.einsum('ed,bdw->bew', Wq, qp) + bq[:, None]
        k = jnp.einsum('ed,bdw->bew', Wk, qp) + bk[:, None]
        val = jnp.einsum('ed,bdw->bew', Wv, vp) + bv[:, None]
        BN = q.shape[0]
        dh = DK // H
        qh = q.reshape(BN, H, dh, W)
        kh = k.reshape(BN, H, dh, W)
        vh = val.reshape(BN, H, dh, W)
        scores = jnp.einsum('bhdi,bhdj->bhij', qh, kh) / jnp.sqrt(jnp.asarray(dh, qh.dtype))
        scores = jnp.where(mp[:, :, None, :] > 0, scores, jnp.asarray(-1000000000.0, scores.dtype))
        attn = jax.nn.softmax(scores, axis=-1)
        o = jnp.einsum('bhij,bhdj->bhdi', attn, vh).reshape(BN, DK, W)
        o = jax.nn.gelu(o, approximate=False)
        out = jnp.einsum('de,bew->bdw', Wo, o) + bo[:, None]
        out = out.reshape(B, np_, D, W).transpose(0, 2, 1, 3).reshape(B, D, S)
        out = out * masks
        return out

    def _L1_ffn_ref(x, W_gate, b_gate, W_e, b_e):
        import jax, jax.numpy as jnp
        import numpy as np
        TOP_K = 2
        logits = x @ W_gate + b_gate
        _, top_idx = jax.lax.top_k(logits, TOP_K)
        y_all = jax.nn.relu(jnp.einsum('bsd,edh->bseh', x, W_e) + b_e)
        y = jnp.take_along_axis(y_all, top_idx[..., None], axis=2)
        return y.mean(axis=2)
    x = x + jnp.tanh(g_xattn[0]) * _L0_xattn_ref(_layernorm(x, axis=-1), ctx_4096, ctx_4096, mask_1x1xSxS2_bk0, L0_xattn_Wq, L0_xattn_Wk, L0_xattn_Wv, L0_xattn_Wo)
    x = x + jnp.tanh(g_ffn[0]) * _L0_ffn_ref(_layernorm(x, axis=-1), L0_ffn_W_base, L0_ffn_b_base, L0_ffn_lora_A, L0_ffn_lora_B, L0_ffn_router_W, L0_ffn_router_b, L0_ffn_domain_prior, L0_ffn_active)
    x = x + jnp.tanh(g_xattn[1]) * _L1_xattn_ref(_layernorm(x, axis=-1), ctx_4096, mask_Bx1x4096_ff1, L1_xattn_Wq, L1_xattn_bq, L1_xattn_Wk, L1_xattn_bk, L1_xattn_Wv, L1_xattn_bv, L1_xattn_Wo, L1_xattn_bo)
    x = x + jnp.tanh(g_ffn[1]) * _L1_ffn_ref(_layernorm(x, axis=-1), L1_ffn_W_gate, L1_ffn_b_gate, L1_ffn_W_e, L1_ffn_b_e)
    return x

_drawn_inputs = setup_inputs


def setup_inputs(seed=0):
    import zlib

    import numpy as np

    out = dict(_drawn_inputs(seed))
    spreads = {'g_ffn': (-1.0, 0.2),
     'L1_xattn_bq': (0.0, 0.332),
     'L1_xattn_bk': (0.0, 2.0),
     'L1_xattn_bv': (0.0, 0.1),
     'L1_xattn_bo': (0.0, 0.1),
     'L1_ffn_b_gate': (0.0, 0.1),
     'L1_ffn_b_e': (0.0, 0.1)}
    factors = {'L0_ffn_router_b': 64.0, 'L0_ffn_domain_prior': 26.983, 'L0_ffn_router_W': 3.041}
    for name, (base, spread) in spreads.items():
        noise = np.random.default_rng([zlib.crc32(name.encode()), seed]).standard_normal(out[name].shape)
        drawn = base * np.exp(spread * noise) if base else spread * noise
        out[name] = jnp.asarray(drawn.astype(out[name].dtype))
    for name, factor in factors.items():
        out[name] = (out[name] * factor).astype(out[name].dtype)
    return out
```

```python
from contextlib import ExitStack

import concourse.bass as bass
from concourse import mybir

F32 = mybir.dt.float32
F32R = mybir.dt.float32r
U8 = mybir.dt.uint8
I32 = mybir.dt.int32
ALU = mybir.AluOpType
ACT = mybir.ActivationFunctionType
AX = mybir.AxisListType

P = 128
B = 8
D = 512
KT = D // P
N = B * P
KV = 8
G = 4
LOGIT_SCALE = 0.08838834764831845
CAP = 30.0
TINY = 2.0**-50
BIG = 1e30
LN_EPS = 1e-5
ET, RANK = 16, 8
H1, DH = 8, 8
E1 = H1 * DH
VA = DH + 1
PATCH = D // P
EX = 8
CREDIT = 2
INV_SQRT_DH = float(1.0 / DH**0.5)


def flamingo_gated_two_layers(nc, x, ctx, ctx_t, mask_tq, mask_b, g_xattn, g_ffn, wq0, wk0, wv0, wo0,
                              wbase_t, bbase, lora_a_t, lora_b, router_t, router_b, prior, active,
                              wq1p, bq1p, wk1p, bk1p, wv1t, bv1, wo1t, bo1, wgate, bgate, we, be,
                              c_ident, c_cos, c_sin, c_aug, c_iota, c_lower, out):
    with ExitStack() as stack:
        def sem(name):
            return stack.enter_context(nc.semaphore(name))

        ARENA = 212_000
        base = (nc.sbuf_base + 31) // 32 * 32
        stack.enter_context(nc.sbuf_tensor("arena", [P, ARENA // 4], F32, align_bytes=32))
        place = [base]

        def sb(name, shape, dt=F32):
            size = 4
            for n in shape[1:]:
                size *= n
            if dt is U8:
                size //= 4
            at = place[0]
            place[0] = at + (size + 31) // 32 * 32
            assert place[0] <= base + ARENA, (name, place[0] - base)
            return nc.alloc_sbuf_tensor_at(name, shape, dt, offset=at)

        X = sb("X", [P, B, D])
        at_xt = place[0]
        xt_hi = sb("xt_hi", [P, KT, N], F32R)
        xt_lo = sb("xt_lo", [P, KT, N], F32R)
        h = sb("h", [P, 2, D])
        ident = sb("ident", [P, P])
        cos = sb("cos", [P, P])
        sin = sb("sin", [P, P])
        mask8 = sb("mask8", [P, P], U8)
        maskf = sb("maskf", [P, P])
        cap = sb("cap", [P, P])
        ones = sb("ones", [P, P])
        tanh_g = sb("tanh_g", [P, 4])
        gates = sb("gates", [P, 4])
        stats = sb("stats", [P, B, 6])
        mean_var = sb("mean_var", [P, B, 2])
        var_eps = sb("var_eps", [P, B])
        rstd = sb("rstd", [P, B])
        minus_half = sb("minus_half", [P, 1])
        denom_inv = sb("denom_inv", [P, 2, G])
        iota = sb("iota", [P, ET])
        active_i = sb("active_i", [P, 4], I32)
        active_f = sb("active_f", [P, 4])
        count = sb("count", [P, 5, ET])
        prior_b = sb("prior_b", [P, ET])
        prior_e = sb("prior_e", [P, ET])
        log_prior = sb("log_prior", [P, ET])
        rb = sb("rb", [P, ET])
        absent = sb("absent", [P, ET])
        absent2 = sb("absent2", [P, ET])
        route_1 = sb("route_1", [P, ET])
        route_bias = sb("route_bias", [P, ET])
        wq1 = sb("wq1", [P, 2, P])
        wk1 = sb("wk1", [P, 2, P])
        wv1 = sb("wv1", [P, E1])
        wo1 = sb("wo1", [E1, P])
        bq1 = sb("bq1", [P, 2])
        bk1 = sb("bk1", [P, 2])
        bv1_b = sb("bv1_b", [P, E1])
        bo1_c = sb("bo1_c", [P, 1])
        aug = sb("aug", [P, 3])
        bq1a = sb("bq1a", [P, 2])
        bk1a = sb("bk1a", [P, 2])
        wg = sb("wg", [P, KT, EX])
        wg_hi = sb("wg_hi", [P, KT, EX], F32R)
        wg_lo = sb("wg_lo", [P, KT, EX], F32R)
        bg = sb("bg", [P, EX])
        lower = sb("lower", [P, EX, EX])

        at_1 = place[0]
        ct_hi = sb("ct_hi", [P, KT, N], F32R)
        ct_lo = sb("ct_lo", [P, KT, N], F32R)
        wq_hi = sb("wq_hi", [P, KT, D], F32R)
        wq_lo = sb("wq_lo", [P, KT, D], F32R)
        wk_hi = sb("wk_hi", [P, KT, P], F32R)
        wk_lo = sb("wk_lo", [P, KT, P], F32R)
        wv_hi = sb("wv_hi", [P, KT, P], F32R)
        wv_lo = sb("wv_lo", [P, KT, P], F32R)
        at_2 = place[0]
        wq_raw = sb("wq_raw", [P, KT, D])
        wk_raw = sb("wk_raw", [P, KT, P])
        wv_raw = sb("wv_raw", [P, KT, P])
        wo_raw = sb("wo_raw", [P, G, D])
        wo_hi = sb("wo_hi", [P, G, D], F32R)
        wo_lo = sb("wo_lo", [P, G, D], F32R)
        q_t = sb("q_t", [P, G, N])
        k_t = sb("k_t", [P, N])
        v_ones = sb("v_ones", [P, B, P + 4])
        e_w = sb("e_w", [P, 2, G * P])
        attn = sb("attn", [P, 2, G * P])
        at_hi = sb("at_hi", [P, 2, G * P], F32R)
        at_lo = sb("at_lo", [P, 2, G * P], F32R)
        rot_a = sb("rot_a", [P, 2, D])
        rot_b = sb("rot_b", [P, 2, D])
        end_2 = place[0]

        place[0] = at_1
        wb_raw = sb("wb_raw", [P, KT, D])
        wb_hi = sb("wb_hi", [P, KT, D], F32R)
        wb_lo = sb("wb_lo", [P, KT, D], F32R)
        ZR = P + ET
        ar_raw = sb("ar_raw", [P, KT, ZR])
        ar_hi = sb("ar_hi", [P, KT, ZR], F32R)
        ar_lo = sb("ar_lo", [P, KT, ZR], F32R)
        lb = sb("lb", [P, D])
        bb = sb("bb", [P, D])
        bbg = sb("bbg", [P, D])
        ht_hi = sb("ht_hi", [P, 2, D], F32R)
        ht_lo = sb("ht_lo", [P, 2, D], F32R)
        t_b = sb("t_b", [P, 2, D])
        z_w = sb("z_w", [P, 2, P])
        z_wt = sb("z_wt", [P, 2, P])
        lg = sb("lg", [P, 2, ET])
        lg_max = sb("lg_max", [P, 2])
        lg_e = sb("lg_e", [P, 2, ET])
        lg_n = sb("lg_n", [P, 2, ET])
        lg_sum = sb("lg_sum", [P, 2])
        lg_inv = sb("lg_inv", [P, 2])
        alpha = sb("alpha", [P, 2, ET])
        assert place[0] <= at_2
        place[0] = at_1
        we_raw = sb("we_raw", [P, 2, KT, D])
        we_hi = [sb(f"we_hi{j}", [P, KT, D], F32R) for j in range(2)]
        we_lo = [sb(f"we_lo{j}", [P, KT, D], F32R) for j in range(2)]
        t_d = sb("t_d", [P, 2, D])
        r_d = sb("r_d", [P, 2, D])
        assert place[0] <= at_2
        place[0] = at_2
        ctx_s = sb("ctx_s", [P, 2, D])
        mask_bb = sb("mask_bb", [P, B, D])
        q_pad = sb("q_pad", [P, 2, 2, D])
        k_raw = sb("k_raw", [P, 2, D])
        m_mul = sb("m_mul", [P, 2, D])
        m_full = sb("m_full", [P, 2, D])
        s_max = sb("s_max", [P, 2, 4])
        s_sub = sb("s_sub", [P, 2, D])
        p_w = sb("p_w", [P, 2, D])
        p_t = sb("p_t", [P, 2, D])
        v_aug = sb("v_aug", [P, 2, PATCH, H1, VA])
        o_inv = sb("o_inv", [P, 2, PATCH * H1])
        o_n = sb("o_n", [P, 2, PATCH * E1])
        o_t = sb("o_t", [E1, B, D])
        t_c = sb("t_c", [P, 2, D])
        be_b = sb("be_b", [P, 2, D])
        gl = sb("gl", [P, B, EX])
        rank_a = sb("rank_a", [P, B, EX, EX])
        rank_b = sb("rank_b", [P, B, EX, EX])
        rank = sb("rank", [P, B, EX])
        sel = sb("sel", [P, B, EX])
        place[0] = at_xt
        k_blk = sb("k_blk", [P, 2, 2, PATCH, 4, P])
        assert place[0] <= at_xt + 8 * KT * N

        ps = stack.enter_context(nc.psum_tensor("ps", [P, 8, 512], F32))

        consts_in, x_in, ctxt_in = sem("consts_in"), [sem(f"x_in{k}") for k in range(4)], sem("ctxt_in")
        wq_in, wk_in, wv_in, wo_in = sem("wq_in"), sem("wk_in"), sem("wv_in"), sem("wo_in")
        ones_ok, prep_v, prep_a, prep_mm = sem("ones_ok"), sem("prep_v"), sem("prep_a"), sem("prep_mm")
        cap_ok, gates_ok = sem("cap_ok"), sem("gates_ok")
        stat_ok, aggr_ok, eps_ok, rstd_ok = sem("stat_ok"), sem("aggr_ok"), sem("eps_ok"), sem("rstd_ok")
        h_ok, ht_mm, hth_ok, htl_ok = sem("h_ok"), sem("ht_mm"), sem("hth_ok"), sem("htl_ok")
        cth_ok, ctl_ok = sem("cth_ok"), sem("ctl_ok")
        qkv_hi_ok, qkv_lo_ok, wo_hi_ok, wo_lo_ok = sem("qkv_hi_ok"), sem("qkv_lo_ok"), sem("wo_hi_ok"), sem("wo_lo_ok")
        proj_mm, rot_ok, rope_ok, v_ok = sem("proj_mm"), sem("rot_ok"), sem("rope_ok"), sem("v_ok")
        s_mm, th_ok, ex_ok, e_ok = sem("s_mm"), sem("th_ok"), sem("ex_ok"), sem("e_ok")
        pv_mm, rec_ok, at_ok, at_mm = sem("pv_mm"), sem("rec_ok"), sem("at_ok"), sem("at_mm")
        ah_ok, al_ok, wo_mm, x1_ok = sem("ah_ok"), sem("al_ok"), sem("wo_mm"), sem("x1_ok")
        wb_in, ar_in, lb_in = sem("wb_in"), sem("ar_in"), sem("lb_in")
        wbh_ok, wbl_ok, bbg_ok = sem("wbh_ok"), sem("wbl_ok"), sem("bbg_ok")
        z_mm, lg_ok, lgm_ok, lge_ok = sem("z_mm"), sem("lg_ok"), sem("lgm_ok"), sem("lge_ok")
        lgs_ok, lgi_ok, al2_ok, zw_ok = sem("lgs_ok"), sem("lgi_ok"), sem("al2_ok"), sem("zw_ok")
        zt_mm, zt_ok, y_mm, tb_ok, x2_ok = sem("zt_mm"), sem("zt_ok"), sem("y_mm"), sem("tb_ok"), sem("x2_ok")
        ctxs_in = [sem("ctxs_in0"), sem("ctxs_in1")]
        maskb_in, kz_ok, va_ok = sem("maskb_in"), sem("kz_ok"), sem("va_ok")
        hc_ok, mm_ok, mf_ok = sem("hc_ok"), sem("mm_ok"), sem("mf_ok")
        pq_mm, pq_ev, cv_ok, kb_ok = sem("pq_mm"), sem("pq_ev"), sem("cv_ok"), sem("kb_ok")
        s2_mm, mx_ok, sb_ok, p_ok = sem("s2_mm"), sem("mx_ok"), sem("sb_ok"), sem("p_ok")
        pt_mm, pt_ok, pv2_mm, oi_ok, on_ok = sem("pt_mm"), sem("pt_ok"), sem("pv2_mm"), sem("oi_ok"), sem("on_ok")
        gelu_ok, c2_mm, tc_ok, x3_ok = sem("gelu_ok"), sem("c2_mm"), sem("tc_ok"), sem("x3_ok")
        we_in = [sem("we_in0"), sem("we_in1")]
        be_in = [sem("be_in0"), sem("be_in1")]
        weh_ok, wel_ok, gate_mm, sel_ok, rank_ok = sem("weh_ok"), sem("wel_ok"), sem("gate_mm"), sem("sel_ok"), sem("rank_ok")
        y2_mm, td_ok, r_ok, x4_ok, out_done = sem("y2_mm"), sem("td_ok"), sem("r_ok"), sem("x4_ok"), sem("out_done")

        N_SMALL = 22
        LAST = KV - 1

        def heads(t):
            return t.rearrange("p (a c) -> p a c", a=4)

        def bcast(t, n):
            return t.unsqueeze(1).to_broadcast([t.shape[0], n, t.shape[-1]])

        def start_counts(engine, semaphores):
            for s in semaphores:
                engine.sem_inc(s, CREDIT)

        block = stack.enter_context(nc.Block())

        @block.sync
        def _(sp):
            def load_qkv(g):
                sp.dma_start(wk_raw[:, :, :], wk0.rearrange("(k p) (g n) -> g p k n", p=P, g=KV)[g]).then_inc(wk_in, 16)
                sp.dma_start(wv_raw[:, :, :], wv0.rearrange("(k p) (g n) -> g p k n", p=P, g=KV)[g]).then_inc(wv_in, 16)
                sp.dma_start(wq_raw[:, :, :], wq0.rearrange("(k p) (g n) -> g p k n", p=P, g=KV)[g]).then_inc(wq_in, 16)

            def load_wo(g):
                sp.dma_start(wo_raw[:, :, :], wo0.rearrange("(g h p) n -> g p h n", p=P, h=G)[g]).then_inc(wo_in, 16)

            ctv = ctx_t.rearrange("(k p) n -> p k n", p=P)
            sp.dma_start(X[:, 0:2, :], x[0:2].rearrange("b t d -> t b d")).then_inc(x_in[0], 16)
            sp.dma_start(q_t[:, :, :], ctv).then_inc(ctxt_in, 16)
            for k in range(1, 4):
                sp.dma_start(X[:, 2 * k:2 * k + 2, :], x[2 * k:2 * k + 2].rearrange("b t d -> t b d")).then_inc(x_in[k], 16)
            load_qkv(0)
            load_wo(0)
            for g in range(1, KV):
                sp.wait_ge(qkv_lo_ok, CREDIT + g * 3)
                load_qkv(g)
                sp.wait_ge(wo_lo_ok, CREDIT + g)
                load_wo(g)
            sp.wait_ge(proj_mm, CREDIT + 12 * KV)
            sp.dma_start(wb_raw[:, :, :], wbase_t.rearrange("(k p) n -> p k n", p=P)).then_inc(wb_in, 16)
            sp.dma_start(ar_raw[:, :, 0:P], lora_a_t.rearrange("(k p) n -> p k n", p=P)).then_inc(ar_in, 16)
            sp.dma_start(ar_raw[:, :, P:ZR], router_t.rearrange("(k p) n -> p k n", p=P)).then_inc(ar_in, 16)
            sp.dma_start(lb[:, :], lora_b).then_inc(lb_in, 16)
            sp.dma_start(bb[:, :], bbase.unsqueeze(0).to_broadcast([P, D])).then_inc(lb_in, 16)
            sp.wait_ge(x1_ok, CREDIT + B * KV)

            def load_ctx(b, j):
                sp.dma_start(ctx_s[:, j, :], ctx[b]).then_inc(ctxs_in[j], 16)

            load_ctx(0, 0)
            load_ctx(1, 1)
            for b in range(B):
                sp.dma_start(mask_bb[:, b, :], mask_b[b, 0:1, :].to_broadcast([P, D])).then_inc(maskb_in, 16)

            def load_expert(e, j):
                sp.dma_start(we_raw[:, j, :, :], we[e].rearrange("(k p) n -> p k n", p=P)).then_inc(we_in[j], 16)
                sp.dma_start(be_b[:, j, :], be[e].unsqueeze(0).to_broadcast([P, D])).then_inc(be_in[j], 16)

            sp.wait_ge(x2_ok, CREDIT + B)
            load_expert(0, 0)
            load_expert(1, 1)
            for b in range(2, B):
                sp.wait_ge(pq_mm, CREDIT + 6 * b - 7)
                load_ctx(b, b % 2)
            for e in range(2, EX):
                sp.wait_ge(wel_ok, CREDIT + 4 * (e - 1))
                sp.wait_ge(td_ok, CREDIT + B * (e - 1))
                load_expert(e, e % 2)
            for b in range(B):
                sp.wait_ge(x4_ok, CREDIT + B * (EX - 1) + 1 + b)
                sp.dma_start(out[b], X[:, b, :]).then_inc(out_done, 16)
            sp.wait_ge(out_done, 16 * B)

        @block.gpsimd
        def _(gp):
            start_counts(gp, (ones_ok, eps_ok, rstd_ok, ctl_ok, qkv_lo_ok, wo_lo_ok, rope_ok, wbl_ok, x2_ok, kz_ok,
                              va_ok, kb_ok, wel_ok))
            nc.gpsimd.memset(minus_half[:, :], -0.5).then_inc(ones_ok, 1)
            nc.gpsimd.memset(ones[:, :], 1.0).then_inc(ones_ok, 1)
            nc.gpsimd.memset(v_ones[:, :, :], 1.0).then_inc(ones_ok, 1)

            def ln_scale(n):
                gp.wait_ge(aggr_ok, CREDIT + B * (n + 1))
                nc.gpsimd.tensor_scalar(var_eps[:, :], mean_var[:, :, 1], LN_EPS, None, ALU.add).then_inc(eps_ok, 1)
                gp.wait_ge(eps_ok, CREDIT + n + 1)
                nc.gpsimd.tensor_tensor(rstd[:, :], var_eps[:, :], minus_half[:, 0:1].to_broadcast([P, B]),
                                        ALU.pow).then_inc(rstd_ok, 1)

            def lo_part(dst, raw, hi, done):
                nc.gpsimd.tensor_tensor(dst, raw, hi.bitcast(F32), ALU.subtract).then_inc(done, 1)

            def qkv_lo(g):
                for n, (lo, raw, hi) in enumerate(((wk_lo, wk_raw, wk_hi), (wv_lo, wv_raw, wv_hi), (wq_lo, wq_raw, wq_hi))):
                    gp.wait_ge(qkv_hi_ok, CREDIT + 3 * g + n + 1)
                    lo_part(lo[:, :, :], raw[:, :, :], hi[:, :, :], qkv_lo_ok)

            gp.wait_ge(ones_ok, CREDIT + 3)
            for k in range(2):
                gp.wait_ge(cth_ok, CREDIT + k + 1)
                lo_part(ct_lo[:, k, :], q_t[:, k, :], ct_hi[:, k, :], ctl_ok)
            qkv_lo(0)
            ln_scale(0)

            def rope_sum(g, r):
                gp.wait_ge(rot_ok, CREDIT + 10 * g + r + 1)
                if r < 2:
                    dst = k_t[:, r * D:(r + 1) * D]
                else:
                    half, head = divmod(r - 2, G)
                    dst = q_t[:, head, half * D:(half + 1) * D]
                nc.gpsimd.tensor_tensor(dst, rot_a[:, r % 2, :], rot_b[:, r % 2, :], ALU.add).then_inc(rope_ok, 1)

            def group(g, more):
                for r in range(6):
                    rope_sum(g, r)
                gp.wait_ge(wo_hi_ok, CREDIT + g + 1)
                lo_part(wo_lo[:, :, :], wo_raw[:, :, :], wo_hi[:, :, :], wo_lo_ok)
                for r in range(6, 10):
                    rope_sum(g, r)
                if more:
                    qkv_lo(g + 1)

            gp.wait_ge(ctl_ok, CREDIT + 4)
            with gp.Fori(0, LAST) as g:
                group(g, True)
            group(LAST, False)

            for k in range(KT):
                gp.wait_ge(wbh_ok, CREDIT + k + 1)
                lo_part(wb_lo[:, k, :], wb_raw[:, k, :], wb_hi[:, k, :], wbl_ok)
            gp.wait_ge(wbh_ok, CREDIT + KT + 1)
            lo_part(ar_lo[:, :, :], ar_raw[:, :, :], ar_hi[:, :, :], wbl_ok)
            nc.gpsimd.memset(k_blk[:, :, :, :, :, :], 0.0).then_inc(kz_ok, 1)
            gp.wait_ge(x1_ok, CREDIT + B * KV)
            nc.gpsimd.memset(v_aug[:, :, :, :, :], 1.0).then_inc(va_ok, 1)
            ln_scale(1)
            with gp.Fori(0, B // 2) as i:
                for j in range(2):
                    gp.wait_ge(tb_ok, CREDIT + 2 * i + j + 1)
                    nc.gpsimd.tensor_tensor(X[:, 2 * i + j, :], X[:, 2 * i + j, :], t_b[:, j, :], ALU.add).then_inc(x2_ok, 1)

            ln_scale(2)

            def kb(b, j, first):
                for grp in range(2):
                    if grp == 0:
                        gp.wait_ge(mf_ok, CREDIT + b + 1)
                    gp.wait_ge(pq_ev, CREDIT + (grp + 1 if first else 5 * b + grp))
                    for hd in range(4):
                        part = slice(32 * hd, 32 * hd + 32)
                        last = nc.gpsimd.tensor_tensor(
                            k_blk[part, j, grp, :, hd, :], heads(k_raw[part, grp, :]), heads(m_full[part, j, :]), ALU.mult)
                    last.then_inc(kb_ok, 1)

            gp.wait_ge(kz_ok, CREDIT + 1)
            kb(0, 0, True)
            kb(1, 1, False)
            with gp.Fori(1, B // 2) as i:
                for j in range(2):
                    kb(2 * i + j, j, False)

            def expert_lo(e, j):
                for k in range(KT):
                    gp.wait_ge(weh_ok, CREDIT + 4 * e + k + 1)
                    lo_part(we_lo[j][:, k, :], we_raw[:, j, k, :], we_hi[j][:, k, :], wel_ok)

            expert_lo(0, 0)
            ln_scale(3)
            with gp.Fori(0, EX // 2 - 1) as i:
                expert_lo(2 * i + 1, 1)
                expert_lo(2 * i + 2, 0)
            expert_lo(EX - 1, 1)

        @block.scalar
        def _(ac):
            small = [
                (ident[:, :], c_ident), (cos[:, :], c_cos), (sin[:, :], c_sin), (mask8[:, :], mask_tq),
                (gates[:, 0:2], g_xattn.unsqueeze(0).to_broadcast([P, 2])),
                (gates[:, 2:4], g_ffn.unsqueeze(0).to_broadcast([P, 2])),
                (iota[:, :], c_iota), (aug[:, :], c_aug), (lower[:, :, :], c_lower),
                (active_i[:, :], active.unsqueeze(0).to_broadcast([P, 4])),
                (prior_b[:, :], prior.unsqueeze(0).to_broadcast([P, ET])),
                (rb[:, :], router_b.unsqueeze(0).to_broadcast([P, ET])),
                (wq1[:, :, :], wq1p), (wk1[:, :, :], wk1p), (bq1[:, :], bq1p), (bk1[:, :], bk1p),
                (wv1[:, :], wv1t), (wo1[:, :], wo1t), (bv1_b[:, :], bv1.unsqueeze(0).to_broadcast([P, E1])),
                (bo1_c[:, :], bo1.unsqueeze(1)), (wg[:, :, :], wgate.rearrange("(k p) e -> p k e", p=P)),
                (bg[:, :], bgate.unsqueeze(0).to_broadcast([P, EX])),
            ]
            assert len(small) == N_SMALL
            for dst, src in small:
                ac.dma_start(dst, src).then_inc(consts_in, 16)
            start_counts(ac, (prep_a, gates_ok, hth_ok, cth_ok, qkv_hi_ok, wo_hi_ok, v_ok, th_ok, ex_ok, ah_ok, wbh_ok,
                              lge_ok, zt_ok, pq_ev, p_ok, pt_ok, gelu_ok, weh_ok, r_ok))

            def hi_part(dst, raw, done):
                nc.scalar.activation(dst, raw, ACT.Copy).then_inc(done, 1)

            ac.wait_ge(ctxt_in, 16)
            for k in range(KT):
                hi_part(ct_hi[:, k, :], q_t[:, k, :], cth_ok)
            for w_in, hi, raw in ((wk_in, wk_hi, wk_raw), (wv_in, wv_hi, wv_raw), (wq_in, wq_hi, wq_raw)):
                ac.wait_ge(w_in, 16)
                hi_part(hi[:, :, :], raw[:, :, :], qkv_hi_ok)
            ac.wait_ge(prep_v, CREDIT + 1)
            nc.scalar.activation(log_prior[:, :], prior_e[:, :], ACT.Ln).then_inc(prep_a, 1)
            nc.scalar.activation(tanh_g[:, :], gates[:, :], ACT.Tanh).then_inc(gates_ok, 1)

            ac.wait_ge(ones_ok, CREDIT + 3)
            with ac.Fori(0, B // 2) as i:
                for j in range(2):
                    ac.wait_ge(ht_mm, CREDIT + 2 * i + j + 1)
                    nc.scalar.activation(xt_hi[:, :, bass.ds((2 * i + j) * P, P)], heads(ps[:, j, :]), ACT.Copy).then_inc(hth_ok, 1)
            ac.wait_ge(gates_ok, CREDIT + 1)

            def group(g, more):
                ac.wait_ge(wo_in, 16 * g + 16)
                ac.wait_ge(wo_mm, CREDIT + B * g)
                hi_part(wo_hi[:, :, :], wo_raw[:, :, :], wo_hi_ok)
                for v in range(2):
                    ac.wait_ge(proj_mm, CREDIT + 12 * g + 3 + v)
                    nc.scalar.activation(v_ones[:, 4 * v:4 * v + 4, 0:P], heads(ps[:, v, :]), ACT.Copy,
                                         scale=tanh_g[:, 0:1]).then_inc(v_ok, 1)

                def weights(b):
                    bank = ps[:, 2 + b % 2, :]
                    ac.wait_ge(s_mm, CREDIT + B * g + b + 1)
                    nc.scalar.activation(bank, bank, ACT.Tanh, scale=LOGIT_SCALE / CAP).then_inc(th_ok, 1)
                    ac.wait_ge(th_ok, CREDIT + B * g + b + 1)
                    nc.scalar.activation(bank, bank, ACT.Exp, scale=CAP).then_inc(ex_ok, 1)

                weights(0)
                weights(1)
                for b in range(B):
                    if b + 2 < B:
                        weights(b + 2)
                    ac.wait_ge(at_mm, CREDIT + B * g + b + 1)
                    ac.wait_ge(wo_mm, CREDIT + B * g + b - 1)
                    nc.scalar.activation(at_hi[:, b % 2, :], ps[:, 6, :], ACT.Copy).then_inc(ah_ok, 1)
                    if more and b in (1, 2, 3):
                        w_in, hi, raw, used = ((wk_in, wk_hi, wk_raw, 2), (wv_in, wv_hi, wv_raw, 4),
                                               (wq_in, wq_hi, wq_raw, 12))[b - 1]
                        ac.wait_ge(w_in, 16 * g + 32)
                        ac.wait_ge(proj_mm, CREDIT + 12 * g + used)
                        hi_part(hi[:, :, :], raw[:, :, :], qkv_hi_ok)

            with ac.Fori(0, LAST) as g:
                group(g, True)
            group(LAST, False)

            ac.wait_ge(wb_in, 16)
            for k in range(KT):
                hi_part(wb_hi[:, k, :], wb_raw[:, k, :], wbh_ok)
            ac.wait_ge(ar_in, 32)
            hi_part(ar_hi[:, :, :], ar_raw[:, :, :], wbh_ok)

            def row_hi(b, j):
                ac.wait_ge(ht_mm, CREDIT + B + b + 1)
                ac.wait_ge(y_mm, CREDIT + b - 1)
                nc.scalar.activation(ht_hi[:, j, :], ps[:, j, :], ACT.Copy).then_inc(hth_ok, 1)

            def mix(b, j, more):
                if more:
                    row_hi(b + 1, 1 - j)
                ac.wait_ge(lgm_ok, CREDIT + b + 1)
                nc.scalar.activation(lg_e[:, j, :], lg[:, j, :], ACT.Exp, bias=lg_max[:, j:j + 1]).then_inc(lge_ok, 1)
                ac.wait_ge(zt_mm, CREDIT + b + 1)
                nc.scalar.activation(z_wt[:, j, :], ps[:, 6, 0:P], ACT.Copy).then_inc(zt_ok, 1)

            ac.wait_ge(ht_mm, CREDIT + B + 1)
            nc.scalar.activation(ht_hi[:, 0, :], ps[:, 0, :], ACT.Copy).then_inc(hth_ok, 1)
            with ac.Fori(0, B // 2 - 1) as i:
                for j in range(2):
                    mix(2 * i + j, j, True)
            mix(B - 2, 0, True)
            mix(B - 1, 1, False)

            def proj_out(b, j, first, what):
                for n, (dst, bias) in enumerate(((k_raw[:, 0, :], bk1a[:, 0:1]), (k_raw[:, 1, :], bk1a[:, 1:2]),
                                                 (q_pad[:, j, 0, :], bq1a[:, 0:1]), (q_pad[:, j, 1, :], bq1a[:, 1:2]))):
                    if n not in what:
                        continue
                    ac.wait_ge(pq_mm, CREDIT + (n + 1 if first else 6 * b + n))
                    if n < 2 and not first:
                        ac.wait_ge(kb_ok, CREDIT + 2 * b - 1 + n)
                    nc.scalar.activation(dst, ps[:, n % 2, :], ACT.Identity, bias=bias).then_inc(pq_ev, 1)

            proj_out(0, 0, True, range(4))

            def batch(b, j, more):
                for u in range(H1):
                    ac.wait_ge(sb_ok, CREDIT + 8 * b + u + 1)
                    ac.wait_ge(pt_mm, CREDIT + 8 * b + u - 1)
                    nc.scalar.activation(p_w[:, u % 2, :], s_sub[:, u % 2, :], ACT.Exp, scale=INV_SQRT_DH).then_inc(p_ok, 1)
                    ac.wait_ge(pt_mm, CREDIT + 8 * b + u + 1)
                    ac.wait_ge(pv2_mm, CREDIT + 8 * b + u - 1)
                    nc.scalar.activation(p_t[:, u % 2, :], ps[:, 4 + u % 2, :], ACT.Copy).then_inc(pt_ok, 1)
                    if more and 1 <= u <= 4:
                        proj_out(b + 1, 1 - j, False, (u - 1,))
                ac.wait_ge(pq_mm, CREDIT + (6 * b + 11 if more else 6 * b + 6))
                nc.scalar.activation(o_t[:, b, :], ps[0:E1, 1, :], ACT.Copy).then_inc(pq_ev, 1)

            with ac.Fori(0, B // 2 - 1) as i:
                for j in range(2):
                    batch(2 * i + j, j, True)
            batch(B - 2, 0, True)
            batch(B - 1, 1, False)
            ac.wait_ge(pq_ev, CREDIT + 5 * B)
            with ac.Fori(0, B) as b:
                nc.scalar.activation(o_t[:, b, :], o_t[:, b, :], ACT.Gelu).then_inc(gelu_ok, 1)

            def expert_hi(e, j, k):
                if k == 0:
                    ac.wait_ge(we_in[j], 8 * (e - j) + 16)
                    ac.wait_ge(y2_mm, CREDIT + B * (e - 1))
                hi_part(we_hi[j][:, k, :], we_raw[:, j, k, :], weh_ok)

            ac.wait_ge(we_in[0], 16)
            for k in range(KT):
                hi_part(we_hi[0][:, k, :], we_raw[:, 0, k, :], weh_ok)
            with ac.Fori(0, B // 2) as i:
                for j in range(2):
                    ac.wait_ge(ht_mm, CREDIT + 2 * B + 2 * i + j + 1)
                    nc.scalar.activation(xt_hi[:, :, bass.ds((2 * i + j) * P, P)], heads(ps[:, j, :]), ACT.Copy).then_inc(hth_ok, 1)
            ac.wait_ge(sel_ok, CREDIT + 1)

            def expert(e, j, more):
                for b in range(B):
                    if more and b < KT:
                        expert_hi(e + 1, 1 - j, b)
                    ac.wait_ge(td_ok, CREDIT + B * e + b + 1)
                    ac.wait_ge(x4_ok, CREDIT + B * e + b - 1)
                    nc.scalar.activation(r_d[:, b % 2, :], t_d[:, b % 2, :], ACT.Relu,
                                         scale=sel[:, b, bass.ds(e, 1)] if not isinstance(e, int) else sel[:, b, e:e + 1]).then_inc(r_ok, 1)

            with ac.Fori(0, EX // 2 - 1) as i:
                for j in range(2):
                    expert(2 * i + j, j, True)
            expert(EX - 2, 0, True)
            expert(EX - 1, 1, False)

        @block.vector
        def _(ve):
            start_counts(ve, (prep_v, cap_ok, stat_ok, aggr_ok, h_ok, htl_ok, rot_ok, e_ok, rec_ok, at_ok, al_ok,
                              x1_ok, bbg_ok, lg_ok, lgm_ok, lgs_ok, lgi_ok, al2_ok, zw_ok, tb_ok, hc_ok, mm_ok, mf_ok,
                              cv_ok, mx_ok, sb_ok, oi_ok, on_ok, tc_ok, x3_ok, sel_ok, rank_ok, td_ok, x4_ok))
            def ln_stats(n, ready, first):
                for b in range(B):
                    ve.wait_ge(ready, CREDIT + b + first)
                    nc.vector.bn_stats(stats[:, b, :], X[:, b, :]).then_inc(stat_ok, 1)
                    ve.wait_ge(stat_ok, CREDIT + B * n + b + 1)
                    nc.vector.bn_aggr(mean_var[:, b, :], stats[:, b, :]).then_inc(aggr_ok, 1)

            def normalise(b, j, done):
                nc.vector.tensor_scalar(h[:, j, :], X[:, b, :], mean_var[:, b, 0:1], rstd[:, bass.ds(b, 1)] if not isinstance(b, int) else rstd[:, b:b + 1],
                                        ALU.subtract, ALU.mult).then_inc(done, 1)

            for b in range(B):
                ve.wait_ge(x_in[b // 2], 16)
                nc.vector.bn_stats(stats[:, b, :], X[:, b, :]).then_inc(stat_ok, 1)
                ve.wait_ge(stat_ok, CREDIT + b + 1)
                nc.vector.bn_aggr(mean_var[:, b, :], stats[:, b, :]).then_inc(aggr_ok, 1)
            for k in range(2, KT):
                ve.wait_ge(cth_ok, CREDIT + k + 1)
                nc.vector.tensor_tensor(ct_lo[:, k, :], q_t[:, k, :], ct_hi[:, k, :].bitcast(F32), ALU.subtract).then_inc(ctl_ok, 1)

            ve.wait_ge(consts_in, 16 * N_SMALL)
            nc.vector.tensor_scalar(prior_e[:, :], prior_b[:, :], 1e-12, None, ALU.add).then_inc(prep_v, 1)
            nc.vector.tensor_copy(active_f[:, :], active_i[:, :]).then_inc(prep_v, 1)
            nc.vector.tensor_copy(maskf[:, :], mask8[:, :]).then_inc(prep_v, 1)
            nc.vector.tensor_copy(wg_hi[:, :, :], wg[:, :, :]).then_inc(prep_v, 1)
            nc.vector.memset(count[:, 0, :], 0.0).then_inc(prep_v, 1)
            nc.vector.tensor_scalar(bq1a[:, :], bq1[:, :], aug[:, 2:3], None, ALU.add).then_inc(prep_v, 1)
            nc.vector.tensor_scalar(bk1a[:, :], bk1[:, :], aug[:, 2:3], None, ALU.add).then_inc(prep_v, 1)
            step = 7
            ve.wait_ge(prep_v, CREDIT + step)
            nc.vector.tensor_tensor(wg_lo[:, :, :], wg[:, :, :], wg_hi[:, :, :].bitcast(F32), ALU.subtract).then_inc(prep_v, 1)
            for k in range(4):
                nc.vector.scalar_tensor_tensor(count[:, k + 1, :], iota[:, :], active_f[:, k:k + 1], count[:, k, :],
                                               ALU.is_equal, ALU.add).then_inc(prep_v, 1)
                ve.wait_ge(prep_v, CREDIT + step + k + 2)
            step += 5
            nc.vector.tensor_scalar(absent[:, :], count[:, 4, :], 0.5, BIG, ALU.is_gt, ALU.mult).then_inc(prep_v, 1)
            ve.wait_ge(prep_a, CREDIT + 1)
            nc.vector.tensor_tensor(route_1[:, :], log_prior[:, :], rb[:, :], ALU.add).then_inc(prep_v, 1)
            ve.wait_ge(prep_v, CREDIT + step + 2)
            nc.vector.tensor_scalar(absent2[:, :], absent[:, :], -BIG, None, ALU.add).then_inc(prep_v, 1)
            ve.wait_ge(prep_v, CREDIT + step + 3)
            nc.vector.tensor_tensor(route_bias[:, :], route_1[:, :], absent2[:, :], ALU.add).then_inc(prep_v, 1)
            ve.wait_ge(prep_mm, CREDIT + 1)
            nc.vector.tensor_scalar(cap[:, :], ps[:, 7, 0:P], 0.5, TINY, ALU.is_lt, ALU.mult).then_inc(prep_v, 1)
            ve.wait_ge(prep_v, CREDIT + step + 5)
            nc.vector.scalar_tensor_tensor(cap[:, :], maskf[:, :], BIG, cap[:, :], ALU.mult, ALU.add).then_inc(cap_ok, 1)

            def transposed(n, hi, lo):
                def lo_of(b, j):
                    ve.wait_ge(hth_ok, CREDIT + B * n + b + 1)
                    nc.vector.tensor_tensor(lo(b), heads(ps[:, j, :]), hi(b).bitcast(F32), ALU.subtract).then_inc(htl_ok, 1)

                with ve.Fori(0, B // 2) as i:
                    for j in range(2):
                        ve.wait_ge(ht_mm, CREDIT + B * n + 2 * i + j - 1)
                        normalise(2 * i + j, j, h_ok)
                    for j in range(2):
                        lo_of(2 * i + j, j)

            def xt(t):
                return lambda b: t[:, :, bass.ds(b * P, P)]

            ve.wait_ge(rstd_ok, CREDIT + 1)
            transposed(0, xt(xt_hi), xt(xt_lo))
            ve.wait_ge(cap_ok, CREDIT + 1)

            def group(g):
                def rotate(r):
                    tile = r if r < 2 else r + 2
                    bank = ps[:, tile % 2, :]
                    ve.wait_ge(proj_mm, CREDIT + 12 * g + tile + 1)
                    ve.wait_ge(rope_ok, CREDIT + 10 * g + r - 1)
                    nc.vector.tensor_tensor(heads(rot_a[:, r % 2, :]), heads(bank), bcast(cos[:, :], 4), ALU.mult)
                    nc.vector.tensor_tensor(heads(rot_b[0:64, r % 2, :]), heads(bank[64:128, :]), bcast(sin[64:128, :], 4), ALU.mult)
                    nc.vector.tensor_tensor(heads(rot_b[64:128, r % 2, :]), heads(bank[0:64, :]), bcast(sin[0:64, :], 4),
                                            ALU.mult).then_inc(rot_ok, 1)

                def mask(b):
                    ve.wait_ge(ex_ok, CREDIT + B * g + b + 1)
                    ve.wait_ge(pv_mm, CREDIT + B * g + b - 1)
                    nc.vector.tensor_tensor(heads(e_w[:, b % 2, :]), heads(ps[:, 2 + b % 2, :]), bcast(cap[:, :], G),
                                            ALU.min).then_inc(e_ok, 1)

                def scale(b):
                    o = ps[:, 4:6, 0:2 * (P + 1)].rearrange("p a (c n) -> p a c n", c=2)
                    inv = denom_inv[:, b % 2, :].rearrange("p (a c) -> p a c", a=2)
                    ve.wait_ge(pv_mm, CREDIT + B * g + b + 1)
                    nc.vector.reciprocal(inv, o[:, :, :, P]).then_inc(rec_ok, 1)
                    ve.wait_ge(rec_ok, CREDIT + B * g + b + 1)
                    ve.wait_ge(at_mm, CREDIT + B * g + b - 1)
                    nc.vector.tensor_tensor(attn[:, b % 2, :].rearrange("p (a c n) -> p a c n", a=2, c=2), o[:, :, :, 0:P],
                                            inv.unsqueeze(3).to_broadcast([P, 2, 2, P]), ALU.mult).then_inc(at_ok, 1)

                def lo_of(b):
                    ve.wait_ge(ah_ok, CREDIT + B * g + b + 1)
                    ve.wait_ge(wo_mm, CREDIT + B * g + b - 1)
                    nc.vector.tensor_tensor(at_lo[:, b % 2, :], ps[:, 6, :], at_hi[:, b % 2, :].bitcast(F32),
                                            ALU.subtract).then_inc(al_ok, 1)

                def add(b):
                    ve.wait_ge(wo_mm, CREDIT + B * g + b + 1)
                    nc.vector.tensor_tensor(X[:, b, :], ps[:, 7, :], X[:, b, :], ALU.add).then_inc(x1_ok, 1)

                for r in range(9):
                    rotate(r)
                mask(0)
                mask(1)
                rotate(9)
                for b in range(B):
                    scale(b)
                    if b >= 1:
                        add(b - 1)
                    if b + 2 < B:
                        mask(b + 2)
                    lo_of(b)
                add(B - 1)

            with ve.Fori(0, KV) as g:
                group(g)

            ve.wait_ge(lb_in, 32)
            ve.wait_ge(gates_ok, CREDIT + 1)
            nc.vector.tensor_scalar(bbg[:, :], bb[:, :], tanh_g[:, 2:3], None, ALU.mult).then_inc(bbg_ok, 1)
            ln_stats(1, x1_ok, B * LAST + 1)
            ve.wait_ge(rstd_ok, CREDIT + 2)
            ve.wait_ge(bbg_ok, CREDIT + 1)

            def mix_lo(b, j):
                ve.wait_ge(hth_ok, CREDIT + B + b + 1)
                nc.vector.tensor_tensor(ht_lo[:, j, :], ps[:, j, :], ht_hi[:, j, :].bitcast(F32), ALU.subtract).then_inc(htl_ok, 1)

            def mix(b, j, more):
                if more:
                    normalise(b + 1, 1 - j, h_ok)
                ve.wait_ge(z_mm, CREDIT + b + 1)
                nc.vector.tensor_tensor(lg[:, j, :], ps[:, 2 + j, P:ZR], route_bias[:, :], ALU.add).then_inc(lg_ok, 1)
                ve.wait_ge(lg_ok, CREDIT + b + 1)
                nc.vector.tensor_reduce(lg_max[:, j:j + 1], lg[:, j, :], AX.X, ALU.max, negate=True).then_inc(lgm_ok, 1)
                if more:
                    mix_lo(b + 1, 1 - j)
                ve.wait_ge(lge_ok, CREDIT + b + 1)
                nc.vector.tensor_tensor_reduce(out=lg_n[:, j, :], in0=lg_e[:, j, :], in1=count[:, 4, :], scale=1.0, scalar=0.0,
                                               op0=ALU.mult, op1=ALU.add, accum_out=lg_sum[:, j:j + 1]).then_inc(lgs_ok, 1)
                ve.wait_ge(lgs_ok, CREDIT + b + 1)
                nc.vector.reciprocal(lg_inv[:, j:j + 1], lg_sum[:, j:j + 1]).then_inc(lgi_ok, 1)
                ve.wait_ge(lgi_ok, CREDIT + b + 1)
                nc.vector.tensor_scalar(alpha[:, j, :], lg_n[:, j, :], lg_inv[:, j:j + 1], 2.0, ALU.mult, ALU.mult).then_inc(al2_ok, 1)
                ve.wait_ge(al2_ok, CREDIT + b + 1)
                nc.vector.tensor_tensor(z_w[:, j, :].rearrange("p (e r) -> p e r", e=ET),
                                        ps[:, 2 + j, 0:P].rearrange("p (e r) -> p e r", e=ET),
                                        alpha[:, j, :].unsqueeze(2).to_broadcast([P, ET, RANK]), ALU.mult).then_inc(zw_ok, 1)
                ve.wait_ge(y_mm, CREDIT + b + 1)
                ve.wait_ge(x2_ok, CREDIT + b - 1)
                nc.vector.scalar_tensor_tensor(t_b[:, j, :], ps[:, 4 + j, :], tanh_g[:, 2:3], bbg[:, :], ALU.mult, ALU.add).then_inc(tb_ok, 1)

            normalise(0, 0, h_ok)
            mix_lo(0, 0)
            with ve.Fori(0, B // 2 - 1) as i:
                for j in range(2):
                    mix(2 * i + j, j, True)
            mix(B - 2, 0, True)
            mix(B - 1, 1, False)

            ln_stats(2, x2_ok, 1)
            ve.wait_ge(rstd_ok, CREDIT + 3)
            ve.wait_ge(maskb_in, 16 * B)

            def rows(b, j):
                normalise(b, j, hc_ok)
                nc.vector.tensor_scalar(m_mul[:, j, :], mask_bb[:, b, :], 0.0, aug[:, 0:1], ALU.is_gt, ALU.mult).then_inc(mm_ok, 1)
                ve.wait_ge(mm_ok, CREDIT + b + 1)
                nc.vector.tensor_scalar(m_full[:, j, :], m_mul[:, j, :], aug[:, 1:2], None, ALU.add).then_inc(mf_ok, 1)

            def values(b, j, first):
                ve.wait_ge(pq_mm, CREDIT + (5 if first else 6 * b + 4))
                nc.vector.tensor_tensor(v_aug[:, j, :, :, 0:DH],
                                        ps[:, 0, 0:PATCH * E1].rearrange("p (a h d) -> p a h d", a=PATCH, h=H1),
                                        bv1_b[:, :].rearrange("p (h d) -> p h d", h=H1).unsqueeze(1).to_broadcast([P, PATCH, H1, DH]),
                                        ALU.add).then_inc(cv_ok, 1)

            rows(0, 0)
            ve.wait_ge(va_ok, CREDIT + 1)
            values(0, 0, True)

            def batch(b, j, more):
                def row_max(u):
                    ve.wait_ge(s2_mm, CREDIT + 8 * b + u + 1)
                    nc.vector.tensor_reduce(s_max[:, u % 2, :], heads(ps[:, 2 + u % 2, :]), AX.X, ALU.max).then_inc(mx_ok, 1)

                def less_max(u):
                    ve.wait_ge(mx_ok, CREDIT + 8 * b + u + 1)
                    ve.wait_ge(p_ok, CREDIT + 8 * b + u - 1)
                    nc.vector.tensor_tensor(heads(s_sub[:, u % 2, :]), heads(ps[:, 2 + u % 2, :]),
                                            s_max[:, u % 2, :].unsqueeze(2).to_broadcast([P, 4, P]), ALU.subtract).then_inc(sb_ok, 1)

                if more:
                    rows(b + 1, 1 - j)
                row_max(0)
                for u in range(H1):
                    if u + 1 < H1:
                        row_max(u + 1)
                    less_max(u)
                    if more and u == 6:
                        values(b + 1, 1 - j, False)
                o = ps[:, 6, 0:PATCH * H1 * VA].rearrange("p (a n) -> p a n", n=VA)
                ve.wait_ge(pv2_mm, CREDIT + 8 * b + 8)
                nc.vector.reciprocal(o_inv[:, j, :], o[:, :, DH]).then_inc(oi_ok, 1)
                ve.wait_ge(oi_ok, CREDIT + b + 1)
                nc.vector.tensor_tensor(o_n[:, j, :].rearrange("p (a d) -> p a d", d=DH), o[:, :, 0:DH],
                                        o_inv[:, j, :].unsqueeze(2).to_broadcast([P, PATCH * H1, DH]), ALU.mult).then_inc(on_ok, 1)

            with ve.Fori(0, B // 2 - 1) as i:
                for j in range(2):
                    batch(2 * i + j, j, True)
            batch(B - 2, 0, True)
            batch(B - 1, 1, False)
            with ve.Fori(0, B // 2) as i:
                for j in range(2):
                    b = 2 * i + j
                    ve.wait_ge(c2_mm, CREDIT + b + 1)
                    nc.vector.scalar_tensor_tensor(t_c[:, j, :], ps[:, 2 + j, :], bo1_c[:, 0:1], mask_bb[:, b, :],
                                                   ALU.add, ALU.mult).then_inc(tc_ok, 1)
                    ve.wait_ge(tc_ok, CREDIT + b + 1)
                    nc.vector.scalar_tensor_tensor(X[:, b, :], t_c[:, j, :], tanh_g[:, 1:2], X[:, b, :],
                                                   ALU.mult, ALU.add).then_inc(x3_ok, 1)

            ln_stats(3, x3_ok, 1)
            ve.wait_ge(rstd_ok, CREDIT + 4)
            transposed(2, xt(xt_hi), xt(xt_lo))
            ve.wait_ge(gate_mm, CREDIT + 1)
            nc.vector.tensor_tensor(gl[:, :, :], ps[:, 2, 0:B * EX].rearrange("p (b e) -> p b e", b=B), bcast(bg[:, :], B), ALU.add).then_inc(rank_ok, 1)
            ve.wait_ge(rank_ok, CREDIT + 1)
            other = gl[:, :, :].unsqueeze(2).to_broadcast([P, B, EX, EX])
            mine = gl[:, :, :].unsqueeze(3).to_broadcast([P, B, EX, EX])
            nc.vector.tensor_tensor(rank_a[:, :, :, :], other, mine, ALU.is_gt).then_inc(rank_ok, 1)
            nc.vector.tensor_tensor(rank_b[:, :, :, :], other, mine, ALU.is_equal).then_inc(rank_ok, 1)
            ve.wait_ge(rank_ok, CREDIT + 3)
            nc.vector.tensor_tensor(rank_b[:, :, :, :], rank_b[:, :, :, :], lower[:, :, :].unsqueeze(1).to_broadcast([P, B, EX, EX]), ALU.mult).then_inc(rank_ok, 1)
            ve.wait_ge(rank_ok, CREDIT + 4)
            nc.vector.tensor_tensor(rank_a[:, :, :, :], rank_a[:, :, :, :], rank_b[:, :, :, :], ALU.add).then_inc(rank_ok, 1)
            ve.wait_ge(rank_ok, CREDIT + 5)
            nc.vector.tensor_reduce(rank[:, :, :], rank_a[:, :, :, :], AX.X, ALU.add).then_inc(rank_ok, 1)
            ve.wait_ge(rank_ok, CREDIT + 6)
            nc.vector.tensor_scalar(sel[:, :, :], rank[:, :, :], 1.5, 0.5, ALU.is_lt, ALU.mult).then_inc(sel_ok, 1)

            def expert(e, j):
                ve.wait_ge(be_in[j], 8 * (e - j) + 16)

                def update(b):
                    ve.wait_ge(r_ok, CREDIT + B * e + b + 1)
                    nc.vector.scalar_tensor_tensor(X[:, b, :], r_d[:, b % 2, :], tanh_g[:, 3:4], X[:, b, :],
                                                   ALU.mult, ALU.add).then_inc(x4_ok, 1)

                for b in range(B):
                    ve.wait_ge(y2_mm, CREDIT + B * e + b + 1)
                    ve.wait_ge(r_ok, CREDIT + B * e + b - 1)
                    nc.vector.tensor_tensor(t_d[:, b % 2, :], ps[:, 4 + b % 2, :], be_b[:, j, :], ALU.add).then_inc(td_ok, 1)
                    if b >= 1:
                        update(b - 1)
                update(B - 1)

            with ve.Fori(0, EX // 2) as i:
                for j in range(2):
                    expert(2 * i + j, j)

        @block.tensor
        def _(pe):
            start_counts(pe, (prep_mm, ht_mm, proj_mm, s_mm, pv_mm, at_mm, wo_mm, z_mm, zt_mm, y_mm, pq_mm, s2_mm,
                              pt_mm, pv2_mm, c2_mm, gate_mm, y2_mm))
            def product(dst, pairs, start=True, stop=True):
                n = len(pairs)
                for k, (w_hi, w_lo, x_hi, x_lo) in enumerate(pairs):
                    nc.tensor.matmul(dst, w_hi, x_hi, start=start and k == 0, stop=False)
                    nc.tensor.matmul(dst, w_hi, x_lo, start=False, stop=False)
                    last = nc.tensor.matmul(dst, w_lo, x_hi, start=False, stop=stop and k == n - 1)
                return last

            def turn_rows(n, b, j):
                pe.wait_ge(h_ok, CREDIT + B * n + b + 1)
                pe.wait_ge(htl_ok, CREDIT + B * n + b - 1)
                for k in range(KT):
                    last = nc.tensor.transpose(ps[:, j, k * P:(k + 1) * P], h[:, j, k * P:(k + 1) * P], ident[:, :])
                last.then_inc(ht_mm, 1)

            pe.wait_ge(ones_ok, CREDIT + 2)
            pe.wait_ge(prep_v, CREDIT + 3)
            pe.wait_ge(consts_in, 16 * N_SMALL)
            nc.tensor.matmul(ps[:, 7, 0:P], ones[:, :], maskf[:, :], start=True, stop=True).then_inc(prep_mm, 1)
            with pe.Fori(0, B // 2) as i:
                for j in range(2):
                    turn_rows(0, 2 * i + j, j)
            pe.wait_ge(ctl_ok, CREDIT + 4)
            pe.wait_ge(htl_ok, CREDIT + B)
            pe.wait_ge(cap_ok, CREDIT + 1)
            pe.wait_ge(ones_ok, CREDIT + 3)

            def group(g):
                def key_tile(half):
                    cols = slice(half * D, (half + 1) * D)
                    product(ps[:, half, :], [(wk_hi[:, k, :], wk_lo[:, k, :], ct_hi[:, k, cols], ct_lo[:, k, cols])
                                             for k in range(KT)]).then_inc(proj_mm, 1)

                def value_tile(half):
                    for c in range(4):
                        rows = slice((4 * half + c) * P, (4 * half + c + 1) * P)
                        last = product(ps[:, half, c * P:(c + 1) * P],
                                       [(ct_hi[:, k, rows], ct_lo[:, k, rows], wv_hi[:, k, :], wv_lo[:, k, :]) for k in range(KT)])
                    last.then_inc(proj_mm, 1)

                def query_tile(q):
                    half, head = divmod(q, G)
                    cols, rows = slice(half * D, (half + 1) * D), slice(head * P, (head + 1) * P)
                    product(ps[:, q % 2, :], [(wq_hi[:, k, rows], wq_lo[:, k, rows], xt_hi[:, k, cols], xt_lo[:, k, cols])
                                              for k in range(KT)]).then_inc(proj_mm, 1)

                def scores(b):
                    if b in (0, 4):
                        pe.wait_ge(rope_ok, CREDIT + 10 * g + 6 + b)
                    pe.wait_ge(e_ok, CREDIT + B * g + b - 1)
                    nc.tensor.matmul(ps[:, 2 + b % 2, :], k_t[:, b * P:(b + 1) * P], q_t[:, :, b * P:(b + 1) * P],
                                     start=True, stop=True).then_inc(s_mm, 1)

                def weighted(b):
                    if b == 0:
                        pe.wait_ge(v_ok, CREDIT + 2 * g + 2)
                    pe.wait_ge(e_ok, CREDIT + B * g + b + 1)
                    pe.wait_ge(at_ok, CREDIT + B * g + b)
                    for n in range(G):
                        at = (n % 2) * (P + 1)
                        last = nc.tensor.matmul(ps[:, 4 + n // 2, at:at + P + 1], e_w[:, b % 2, n * P:(n + 1) * P],
                                                v_ones[:, b, 0:P + 1], start=True, stop=True)
                    last.then_inc(pv_mm, 1)

                def turn(b):
                    pe.wait_ge(at_ok, CREDIT + B * g + b + 1)
                    pe.wait_ge(al_ok, CREDIT + B * g + b)
                    for n in range(G):
                        last = nc.tensor.transpose(ps[:, 6, n * P:(n + 1) * P], attn[:, b % 2, n * P:(n + 1) * P], ident[:, :])
                    last.then_inc(at_mm, 1)

                def output(b):
                    if b == 0:
                        pe.wait_ge(wo_lo_ok, CREDIT + g + 1)
                    pe.wait_ge(al_ok, CREDIT + B * g + b + 1)
                    pe.wait_ge(x1_ok, CREDIT + B * g + b)
                    product(ps[:, 7, :], [(at_hi[:, b % 2, n * P:(n + 1) * P], at_lo[:, b % 2, n * P:(n + 1) * P],
                                           wo_hi[:, n, :], wo_lo[:, n, :]) for n in range(G)]).then_inc(wo_mm, 1)

                pe.wait_ge(rot_ok, CREDIT + 10 * g)
                pe.wait_ge(qkv_lo_ok, CREDIT + 3 * g + 1)
                key_tile(0)
                key_tile(1)
                pe.wait_ge(qkv_lo_ok, CREDIT + 3 * g + 2)
                for half in range(2):
                    pe.wait_ge(rot_ok, CREDIT + 10 * g + half + 1)
                    value_tile(half)
                pe.wait_ge(qkv_lo_ok, CREDIT + 3 * g + 3)
                for q in range(8):
                    if q < 2:
                        pe.wait_ge(v_ok, CREDIT + 2 * g + q + 1)
                    else:
                        pe.wait_ge(rot_ok, CREDIT + 10 * g + q + 1)
                    query_tile(q)
                    if q == 5:
                        scores(0)
                        scores(1)
                for b in range(B):
                    weighted(b)
                    if b + 2 < B:
                        scores(b + 2)
                    if b >= 1:
                        output(b - 1)
                    turn(b)
                output(B - 1)

            with pe.Fori(0, KV) as g:
                group(g)

            pe.wait_ge(wbl_ok, CREDIT + KT + 1)
            pe.wait_ge(lb_in, 32)

            def mix(b, j, more):
                if more:
                    turn_rows(1, b + 1, 1 - j)
                pe.wait_ge(htl_ok, CREDIT + B + b + 1)
                pe.wait_ge(zw_ok, CREDIT + b - 1)
                pe.wait_ge(tb_ok, CREDIT + b - 1)
                rows = [(ht_hi[:, j, k * P:(k + 1) * P], ht_lo[:, j, k * P:(k + 1) * P]) for k in range(KT)]
                product(ps[:, 2 + j, 0:ZR], [(*rows[k], ar_hi[:, k, :], ar_lo[:, k, :]) for k in range(KT)]).then_inc(z_mm, 1)
                product(ps[:, 4 + j, :], [(*rows[k], wb_hi[:, k, :], wb_lo[:, k, :]) for k in range(KT)], stop=False)
                pe.wait_ge(zw_ok, CREDIT + b + 1)
                pe.wait_ge(zt_ok, CREDIT + b)
                nc.tensor.transpose(ps[:, 6, 0:P], z_w[:, j, :], ident[:, :]).then_inc(zt_mm, 1)
                pe.wait_ge(zt_ok, CREDIT + b + 1)
                nc.tensor.matmul(ps[:, 4 + j, :], z_wt[:, j, :], lb[:, :], start=False, stop=True).then_inc(y_mm, 1)

            turn_rows(1, 0, 0)
            with pe.Fori(0, B // 2 - 1) as i:
                for j in range(2):
                    mix(2 * i + j, j, True)
            mix(B - 2, 0, True)
            mix(B - 1, 1, False)

            def proj(b, j, first, n):
                if n == 0:
                    pe.wait_ge(hc_ok, CREDIT + b + 1)
                if not first or n >= 2:
                    if n == 0:
                        pe.wait_ge(cv_ok, CREDIT + b)
                    else:
                        pe.wait_ge(pq_ev, CREDIT + (n - 1 if first else 5 * b - 2 + n))
                if n < 4:
                    w = (wk1, wk1, wq1, wq1)[n]
                    last = nc.tensor.matmul(ps[:, n % 2, :], w[:, n % 2, :], h[:, j, :], start=True, stop=True)
                else:
                    pe.wait_ge(ctxs_in[j], 8 * (b - j) + 16)
                    for a in range(PATCH):
                        last = nc.tensor.matmul(ps[:, 0, a * E1:(a + 1) * E1], ctx_s[:, j, a * P:(a + 1) * P], wv1[:, :], start=True, stop=True)
                last.then_inc(pq_mm, 1)

            def scores(u, j, wait):
                wait()
                nc.tensor.matmul(ps[:, 2 + u % 2, :], q_pad[:, j, u % 2, (u // 2) * P:(u // 2 + 1) * P],
                                 k_blk[:, j, u % 2, u // 2, :, :], start=True, stop=True).then_inc(s2_mm, 1)

            def batch(b, j, more):
                def turn(u):
                    pe.wait_ge(p_ok, CREDIT + 8 * b + u + 1)
                    pe.wait_ge(pt_ok, CREDIT + 8 * b + u - 1)
                    for n in range(4):
                        last = nc.tensor.transpose(ps[:, 4 + u % 2, n * P:(n + 1) * P], p_w[:, u % 2, n * P:(n + 1) * P], ident[:, :])
                    last.then_inc(pt_mm, 1)

                def weighted(u):
                    patch, grp = divmod(u, 2)
                    pe.wait_ge(pt_ok, CREDIT + 8 * b + u + 1)
                    for n in range(4):
                        head = 4 * grp + n
                        at = (patch * H1 + head) * VA
                        last = nc.tensor.matmul(ps[:, 6, at:at + VA], p_t[:, u % 2, n * P:(n + 1) * P], v_aug[:, j, patch, head, :],
                                                start=True, stop=True)
                    last.then_inc(pv2_mm, 1)

                for u in range(H1):
                    if u + 2 < H1:
                        scores(u + 2, j, lambda: pe.wait_ge(sb_ok, CREDIT + 8 * b + u + 1))
                    elif more and u == 6:
                        pe.wait_ge(kb_ok, CREDIT + 2 * b + 3)
                        pe.wait_ge(pq_ev, CREDIT + 5 * b + 7)
                        scores(0, 1 - j, lambda: pe.wait_ge(sb_ok, CREDIT + 8 * b + 7))
                    turn(u)
                    if u == 0:
                        pe.wait_ge(cv_ok, CREDIT + b + 1)
                    if u >= 1:
                        weighted(u - 1)
                    if more and 1 <= u <= 5:
                        proj(b + 1, 1 - j, False, u - 1)
                if more:
                    pe.wait_ge(kb_ok, CREDIT + 2 * b + 4)
                    pe.wait_ge(pq_ev, CREDIT + 5 * b + 8)
                    scores(1, 1 - j, lambda: pe.wait_ge(sb_ok, CREDIT + 8 * b + 8))
                weighted(7)
                pe.wait_ge(on_ok, CREDIT + b + 1)
                pe.wait_ge(pq_ev, CREDIT + (5 * b + 8 if more else 5 * b + 4))
                for a in range(PATCH):
                    last = nc.tensor.matmul(ps[0:E1, 1, a * P:(a + 1) * P], o_n[:, j, a * E1:(a + 1) * E1], ident[:, :],
                                            start=True, stop=True)
                last.then_inc(pq_mm, 1)

            for n in range(5):
                proj(0, 0, True, n)
            pe.wait_ge(kb_ok, CREDIT + 1)
            scores(0, 0, lambda: pe.wait_ge(pq_ev, CREDIT + 3))
            pe.wait_ge(kb_ok, CREDIT + 2)
            scores(1, 0, lambda: pe.wait_ge(pq_ev, CREDIT + 4))
            with pe.Fori(0, B // 2 - 1) as i:
                for j in range(2):
                    batch(2 * i + j, j, True)
            batch(B - 2, 0, True)
            batch(B - 1, 1, False)
            with pe.Fori(0, B // 2) as i:
                for j in range(2):
                    b = 2 * i + j
                    pe.wait_ge(gelu_ok, CREDIT + b + 1)
                    pe.wait_ge(tc_ok, CREDIT + b - 1)
                    nc.tensor.matmul(ps[:, 2 + j, :], wo1[:, :], o_t[:, b, :], start=True, stop=True).then_inc(c2_mm, 1)

            with pe.Fori(0, B // 2) as i:
                for j in range(2):
                    turn_rows(2, 2 * i + j, j)

            def row_tiles(b):
                return [(xt_hi[:, k, b * P:(b + 1) * P], xt_lo[:, k, b * P:(b + 1) * P]) for k in range(KT)]

            pe.wait_ge(htl_ok, CREDIT + 3 * B)
            for b in range(B):
                last = product(ps[:, 2, b * EX:(b + 1) * EX], [(*row_tiles(b)[k], wg_hi[:, k, :], wg_lo[:, k, :]) for k in range(KT)])
            last.then_inc(gate_mm, 1)

            def expert(e, j):
                pe.wait_ge(wel_ok, CREDIT + 4 * e + 4)
                for b in range(B):
                    pe.wait_ge(td_ok, CREDIT + B * e + b - 1)
                    product(ps[:, 4 + b % 2, :], [(*row_tiles(b)[k], we_hi[j][:, k, :], we_lo[j][:, k, :]) for k in range(KT)]).then_inc(y2_mm, 1)

            with pe.Fori(0, EX // 2) as i:
                for j in range(2):
                    expert(2 * i + j, j)


def _constants():
    import numpy as np

    inv_freq = np.float32(1.0) / np.float32(10000.0) ** (np.arange(0, P, 2, dtype=np.float32) / np.float32(P))
    phase = np.arange(P, dtype=np.float32)[None, :] * np.tile(inv_freq, 2)[:, None]
    sin = np.sin(phase)
    sin[P // 2:] *= -1.0
    aug = np.zeros((P, 3), np.float32)
    row = np.arange(P) % 32
    penalty = np.float32(1e9 * DH**0.5)
    aug[:, 0] = np.where(row == DH, penalty, 1.0)
    aug[:, 1] = np.where(row == DH, -penalty, 0.0)
    aug[:, 2] = row == DH
    lower = np.broadcast_to(np.tril(np.ones((EX, EX), np.float32), -1), (P, EX, EX))
    return {
        "ident": np.eye(P, dtype=np.float32), "cos": np.cos(phase).astype(np.float32), "sin": sin.astype(np.float32),
        "aug": aug, "iota": np.broadcast_to(np.arange(ET, dtype=np.float32), (P, ET)), "lower": lower,
    }


def kernel(x, ctx_4096, mask_1x1xSxS2_bk0, mask_Bx1x4096_ff1, g_xattn, g_ffn, L0_xattn_Wq, L0_xattn_Wk, L0_xattn_Wv,
           L0_xattn_Wo, L0_ffn_W_base, L0_ffn_b_base, L0_ffn_lora_A, L0_ffn_lora_B, L0_ffn_router_W, L0_ffn_router_b,
           L0_ffn_domain_prior, L0_ffn_active, L1_xattn_Wq, L1_xattn_bq, L1_xattn_Wk, L1_xattn_bk, L1_xattn_Wv,
           L1_xattn_bv, L1_xattn_Wo, L1_xattn_bo, L1_ffn_W_gate, L1_ffn_b_gate, L1_ffn_W_e, L1_ffn_b_e):
    import concourse.bacc as bacc
    import numpy as np
    from concourse.bass_utils import run_bass_kernel_spmd

    def pad_heads(w):
        w = np.asarray(w)
        wide = np.zeros(w.shape[:-1] + (2, 4, 32), w.dtype)
        wide[..., :DH] = w.reshape(w.shape[:-1] + (2, 4, DH))
        return wide.reshape(w.shape[:-1] + (2, P))

    c = _constants()
    arrays = [
        ("x", x), ("ctx", ctx_4096), ("ctx_t", np.asarray(ctx_4096).reshape(N, D).T),
        ("mask_tq", np.asarray(mask_1x1xSxS2_bk0)[0, 0].T), ("mask_b", mask_Bx1x4096_ff1),
        ("g_xattn", g_xattn), ("g_ffn", g_ffn), ("wq0", L0_xattn_Wq), ("wk0", L0_xattn_Wk), ("wv0", L0_xattn_Wv),
        ("wo0", L0_xattn_Wo), ("wbase_t", np.asarray(L0_ffn_W_base).T), ("bbase", L0_ffn_b_base),
        ("lora_a_t", np.asarray(L0_ffn_lora_A).reshape(ET * RANK, D).T),
        ("lora_b", np.asarray(L0_ffn_lora_B).transpose(0, 2, 1).reshape(ET * RANK, D)),
        ("router_t", np.asarray(L0_ffn_router_W).T), ("router_b", L0_ffn_router_b), ("prior", L0_ffn_domain_prior),
        ("active", L0_ffn_active),
        ("wq1p", pad_heads(np.asarray(L1_xattn_Wq).T)), ("bq1p", pad_heads(L1_xattn_bq).T),
        ("wk1p", pad_heads(np.asarray(L1_xattn_Wk).T)), ("bk1p", pad_heads(L1_xattn_bk).T),
        ("wv1t", np.asarray(L1_xattn_Wv).T), ("bv1", L1_xattn_bv), ("wo1t", np.asarray(L1_xattn_Wo).T), ("bo1", L1_xattn_bo),
        ("wgate", L1_ffn_W_gate), ("bgate", L1_ffn_b_gate), ("we", L1_ffn_W_e), ("be", L1_ffn_b_e),
        ("c_ident", c["ident"]), ("c_cos", c["cos"]), ("c_sin", c["sin"]), ("c_aug", c["aug"]), ("c_iota", c["iota"]),
        ("c_lower", c["lower"]),
    ]
    nc = bacc.Bacc("TRN2", target_bir_lowering=False, num_devices=1)
    feed, args = {}, []
    for name, a in arrays:
        a = np.ascontiguousarray(a)
        feed["in_" + name] = a
        args.append(nc.dram_tensor("in_" + name, a.shape, mybir.dt.from_np(a.dtype), kind="ExternalInput").ap())
    args.append(nc.dram_tensor("out_x", (B, P, D), F32, kind="ExternalOutput").ap())
    flamingo_gated_two_layers(nc, *args)
    return run_bass_kernel_spmd(nc, [feed], core_ids=[0]).results[0]["out_x"]
```

```python
from contextlib import ExitStack

import concourse.bass as bass
from concourse import mybir

F32 = mybir.dt.float32
F32R = mybir.dt.float32r
U8 = mybir.dt.uint8
I32 = mybir.dt.int32
ALU = mybir.AluOpType
ACT = mybir.ActivationFunctionType
AX = mybir.AxisListType

P = 128
B = 8
D = 512
KT = D // P
N = B * P
KV = 8
G = 4
LOGIT_SCALE = 0.08838834764831845
CAP = 30.0
TINY = 2.0**-50
BIG = 1e30
LN_EPS = 1e-5
ET, RANK = 16, 8
H1, DH = 8, 8
E1 = H1 * DH
VA = DH + 1
PATCH = D // P
EX = 8
CREDIT = 4
INV_SQRT_DH = float(1.0 / DH**0.5)


def flamingo_gated_two_layers(nc, x, ctx, ctx_t, mask_tq, mask_b, g_xattn, g_ffn, wq0, wk0, wv0, wo0,
                              wbase_t, bbase, lora_a_t, lora_b, router_t, router_b, prior, active,
                              wq1p, bq1p, wk1p, bk1p, wv1t, bv1, wo1t, bo1, wgate, bgate, we, be,
                              c_ident, c_cos, c_sin, c_aug, c_iota, c_lower, out):
    with ExitStack() as stack:
        def sem(name):
            return stack.enter_context(nc.semaphore(name))

        ARENA = 212_000
        base = (nc.sbuf_base + 31) // 32 * 32
        stack.enter_context(nc.sbuf_tensor("arena", [P, ARENA // 4], F32, align_bytes=32))
        place = [base]

        def sb(name, shape, dt=F32):
            size = 4
            for n in shape[1:]:
                size *= n
            if dt is U8:
                size //= 4
            at = place[0]
            place[0] = at + (size + 31) // 32 * 32
            assert place[0] <= base + ARENA, (name, place[0] - base)
            return nc.alloc_sbuf_tensor_at(name, shape, dt, offset=at)

        def over(name, shape):
            at = place[0]
            raw = sb(name, shape)
            place[0] = at
            return raw

        X = sb("X", [P, B, D])
        at_xt = place[0]
        xt_hi = sb("xt_hi", [P, KT, N], F32R)
        xt_lo = sb("xt_lo", [P, KT, N], F32R)
        h = sb("h", [P, 2, D])
        ident = sb("ident", [P, P])
        cos = sb("cos", [P, P])
        sin = sb("sin", [P, P])
        mask8 = sb("mask8", [P, P], U8)
        maskf = sb("maskf", [P, P])
        cap = sb("cap", [P, P])
        ones = sb("ones", [P, P])
        tanh_g = sb("tanh_g", [P, 4])
        gates = sb("gates", [P, 4])
        stats = sb("stats", [P, 2, 6])
        mean_var = sb("mean_var", [P, 2, 2])
        var_eps = sb("var_eps", [P, 2])
        mean = sb("mean", [P, B])
        rstd = sb("rstd", [P, B])
        minus_half = sb("minus_half", [P, 1])
        ln_eps = sb("ln_eps", [P, 1])
        denom_inv = sb("denom_inv", [P, 2, G])
        iota = sb("iota", [P, ET])
        active_i = sb("active_i", [P, 4], I32)
        active_f = sb("active_f", [P, 4])
        count = sb("count", [P, 5, ET])
        prior_b = sb("prior_b", [P, ET])
        prior_e = sb("prior_e", [P, ET])
        log_prior = sb("log_prior", [P, ET])
        rb = sb("rb", [P, ET])
        absent = sb("absent", [P, ET])
        absent2 = sb("absent2", [P, ET])
        route_1 = sb("route_1", [P, ET])
        route_bias = sb("route_bias", [P, ET])
        wq1 = sb("wq1", [P, 2, P])
        wk1 = sb("wk1", [P, 2, P])
        wv1 = sb("wv1", [P, E1])
        wo1 = sb("wo1", [E1, P])
        bq1 = sb("bq1", [P, 2])
        bk1 = sb("bk1", [P, 2])
        bv1_b = sb("bv1_b", [P, E1])
        bo1_c = sb("bo1_c", [P, 1])
        aug = sb("aug", [P, 3])
        bq1a = sb("bq1a", [P, 2])
        bk1a = sb("bk1a", [P, 2])
        wo1g = sb("wo1g", [E1, P])
        bo1g = sb("bo1g", [P, 1])
        wg = sb("wg", [P, KT, EX])
        wg_hi = sb("wg_hi", [P, KT, EX], F32R)
        wg_lo = sb("wg_lo", [P, KT, EX], F32R)
        bg = sb("bg", [P, EX])
        lower = sb("lower", [P, EX, EX])

        at_1 = place[0]
        ct_hi = sb("ct_hi", [P, KT, N], F32R)
        ct_lo = sb("ct_lo", [P, KT, N], F32R)
        wq_hi = sb("wq_hi", [P, KT, D], F32R)
        wq_raw = over("wq_raw", [P, KT, D])
        wq_lo = sb("wq_lo", [P, KT, D], F32R)
        wk_hi = sb("wk_hi", [P, KT, P], F32R)
        wk_raw = over("wk_raw", [P, KT, P])
        wk_lo = sb("wk_lo", [P, KT, P], F32R)
        wv_hi = sb("wv_hi", [P, KT, 2 * P], F32R)
        wv_raw = over("wv_raw", [P, KT, 2 * P])
        wv_lo = sb("wv_lo", [P, KT, 2 * P], F32R)
        at_2 = place[0]
        wo_raw = sb("wo_raw", [P, G, D])
        wo_hi = sb("wo_hi", [P, G, D], F32R)
        wo_lo = sb("wo_lo", [P, G, D], F32R)
        q_t = sb("q_t", [P, G, N])
        k_t = sb("k_t", [P, N])
        v_ones = sb("v_ones", [P, B, 2, P + 4])
        e_w = sb("e_w", [P, 2, G * P])
        attn = sb("attn", [P, 2, G * P])
        at_hi = sb("at_hi", [P, 2, G * P], F32R)
        at_lo = sb("at_lo", [P, 2, G * P], F32R)
        rot_a = sb("rot_a", [P, 2, D])
        rot_b = sb("rot_b", [P, 2, D])
        end_2 = place[0]

        place[0] = at_1
        wb_raw = sb("wb_raw", [P, KT, D])
        wb_hi = sb("wb_hi", [P, KT, D], F32R)
        wb_lo = sb("wb_lo", [P, KT, D], F32R)
        ZR = P + ET
        ar_raw = sb("ar_raw", [P, KT, ZR])
        ar_hi = sb("ar_hi", [P, KT, ZR], F32R)
        ar_lo = sb("ar_lo", [P, KT, ZR], F32R)
        lb = sb("lb", [P, D])
        bb = sb("bb", [P, D])
        bbg = sb("bbg", [P, D])
        ht_hi = sb("ht_hi", [P, 2, D], F32R)
        ht_lo = sb("ht_lo", [P, 2, D], F32R)
        t_b = sb("t_b", [P, 2, D])
        z_w = sb("z_w", [P, 2, P])
        z_wt = sb("z_wt", [P, 2, P])
        lg = sb("lg", [P, 2, ET])
        lg_max = sb("lg_max", [P, 2])
        lg_e = sb("lg_e", [P, 2, ET])
        lg_n = sb("lg_n", [P, 2, ET])
        lg_sum = sb("lg_sum", [P, 2])
        lg_inv = sb("lg_inv", [P, 2])
        alpha = sb("alpha", [P, 2, ET])
        assert place[0] <= at_2
        place[0] = at_1
        we_raw = sb("we_raw", [P, 2, KT, D])
        we_hi = [sb(f"we_hi{j}", [P, KT, D], F32R) for j in range(2)]
        we_lo = [sb(f"we_lo{j}", [P, KT, D], F32R) for j in range(2)]
        t_d = sb("t_d", [P, 2, D])
        r_d = sb("r_d", [P, 2, D])
        assert place[0] <= at_2
        place[0] = at_2
        ctx_s = sb("ctx_s", [P, 2, D])
        mask_bb = sb("mask_bb", [P, B, D])
        q_pad = sb("q_pad", [P, 2, 2, D])
        k_raw = sb("k_raw", [P, 2, D])
        m_mul = sb("m_mul", [P, 2, D])
        m_full = sb("m_full", [P, 2, D])
        s_max = sb("s_max", [P, 2, 4])
        s_sub = sb("s_sub", [P, 2, D])
        p_w = sb("p_w", [P, 2, D])
        p_t = sb("p_t", [P, 2, D])
        v_aug = sb("v_aug", [P, 2, PATCH, H1, VA])
        o_inv = sb("o_inv", [P, 2, PATCH * H1])
        o_n = sb("o_n", [P, 2, PATCH * E1])
        o_t = sb("o_t", [E1, B, D])
        t_c = sb("t_c", [P, 2, D])
        be_b = sb("be_b", [P, 2, D])
        gl = sb("gl", [P, B, EX])
        rank_a = sb("rank_a", [P, B, EX, EX])
        rank_b = sb("rank_b", [P, B, EX, EX])
        rank = sb("rank", [P, B, EX])
        sel = sb("sel", [P, B, EX])
        place[0] = at_xt
        k_blk = sb("k_blk", [P, 2, 2, PATCH, 4, P])
        assert place[0] <= at_xt + 8 * KT * N

        ps = stack.enter_context(nc.psum_tensor("ps", [P, 8, 512], F32))

        consts_in, x_in, ctxt_in = sem("consts_in"), [sem(f"x_in{k}") for k in range(4)], [sem(f"ctxt_in{k}") for k in range(2)]
        wq_in, wk_in, wv_in, wo_in = sem("wq_in"), sem("wk_in"), sem("wv_in"), sem("wo_in")
        ones_ok, prep_v, prep_a, prep_mm = sem("ones_ok"), sem("prep_v"), sem("prep_a"), sem("prep_mm")
        cap_ok, gates_ok = sem("cap_ok"), sem("gates_ok")
        stat_ok, aggr_ok, eps_ok, rstd_ok = sem("stat_ok"), sem("aggr_ok"), sem("eps_ok"), sem("rstd_ok")
        h_ok, ht_mm, hth_ok, htl_ok = sem("h_ok"), sem("ht_mm"), sem("hth_ok"), sem("htl_ok")
        cth_ok, ctl_ok = sem("cth_ok"), sem("ctl_ok")
        wkh_ok, wkl_ok, wvh_ok, wvl_ok = sem("wkh_ok"), sem("wkl_ok"), sem("wvh_ok"), sem("wvl_ok")
        wqh_ok, wql_ok, wo_hi_ok, wo_lo_ok = sem("wqh_ok"), sem("wql_ok"), sem("wo_hi_ok"), sem("wo_lo_ok")
        kp_mm, vp_mm, qp_mm, rot_ok, rope_ok, v_ok = sem("kp_mm"), sem("vp_mm"), sem("qp_mm"), sem("rot_ok"), sem("rope_ok"), sem("v_ok")
        s_mm, th_ok, ex_ok, e_ok = sem("s_mm"), sem("th_ok"), sem("ex_ok"), sem("e_ok")
        pv_mm, rec_ok, at_ok, at_mm = sem("pv_mm"), sem("rec_ok"), sem("at_ok"), sem("at_mm")
        ah_ok, al_ok, wo_mm, x1_ok = sem("ah_ok"), sem("al_ok"), sem("wo_mm"), sem("x1_ok")
        wb_in, ar_in, lb_in = sem("wb_in"), sem("ar_in"), sem("lb_in")
        wbh_ok, wbl_ok, bbg_ok = sem("wbh_ok"), sem("wbl_ok"), sem("bbg_ok")
        z_mm, lg_ok, lgm_ok, lge_ok = sem("z_mm"), sem("lg_ok"), sem("lgm_ok"), sem("lge_ok")
        lgs_ok, lgi_ok, al2_ok, zw_ok = sem("lgs_ok"), sem("lgi_ok"), sem("al2_ok"), sem("zw_ok")
        zt_mm, zt_ok, yb_mm, y_mm, tb_ok, x2_ok = sem("zt_mm"), sem("zt_ok"), sem("yb_mm"), sem("y_mm"), sem("tb_ok"), sem("x2_ok")
        ctxs_in = [sem("ctxs_in0"), sem("ctxs_in1")]
        maskb_in, kz_ok, va_ok = sem("maskb_in"), sem("kz_ok"), sem("va_ok")
        hc_ok, mm_ok, mf_ok = sem("hc_ok"), sem("mm_ok"), sem("mf_ok")
        pq_mm, pq_ev, cv_ok, kb_ok = sem("pq_mm"), sem("pq_ev"), sem("cv_ok"), sem("kb_ok")
        s2_mm, mx_ok, sb_ok, p_ok = sem("s2_mm"), sem("mx_ok"), sem("sb_ok"), sem("p_ok")
        wo1_ok, ot_mm, ot_ev = sem("wo1_ok"), sem("ot_mm"), sem("ot_ev")
        pt_mm, pt_ok, pv2_mm, oi_ok, on_ok = sem("pt_mm"), sem("pt_ok"), sem("pv2_mm"), sem("oi_ok"), sem("on_ok")
        gelu_ok, c2_mm, tc_ok, x3_ok = sem("gelu_ok"), sem("c2_mm"), sem("tc_ok"), sem("x3_ok")
        we_in = [sem("we_in0"), sem("we_in1")]
        be_in = [sem("be_in0"), sem("be_in1")]
        weh_ok, wel_ok, gate_mm, sel_ok, rank_ok = sem("weh_ok"), sem("wel_ok"), sem("gate_mm"), sem("sel_ok"), sem("rank_ok")
        y2_mm, td_ok, r_ok, x4_ok, out_done = sem("y2_mm"), sem("td_ok"), sem("r_ok"), sem("x4_ok"), sem("out_done")

        N_SMALL = 22
        LAST = KV - 1
        PAIRS = KV // 2
        HALF = N // 2

        def heads(t):
            return t.rearrange("p (a c) -> p a c", a=4)

        def bcast(t, n):
            return t.unsqueeze(1).to_broadcast([t.shape[0], n, t.shape[-1]])

        def start_counts(engine, semaphores):
            for s in semaphores:
                engine.sem_inc(s, CREDIT)

        block = stack.enter_context(nc.Block())

        @block.sync
        def _(sp):
            def load_wk(g):
                sp.dma_start(wk_raw[:, :, :], wk0.rearrange("(k p) (g n) -> g p k n", p=P, g=KV)[g]).then_inc(wk_in, 16)

            def load_wv(p):
                sp.dma_start(wv_raw[:, :, :], wv0.rearrange("(k p) (g n) -> g p k n", p=P, g=PAIRS)[p]).then_inc(wv_in, 16)

            def load_wq(g):
                sp.dma_start(wq_raw[:, :, :], wq0.rearrange("(k p) (g n) -> g p k n", p=P, g=KV)[g]).then_inc(wq_in, 16)

            def load_wo(g):
                sp.dma_start(wo_raw[:, :, :], wo0.rearrange("(g h p) n -> g p h n", p=P, h=G)[g]).then_inc(wo_in, 16)

            ctv = ctx_t.rearrange("(k p) n -> p k n", p=P)
            sp.dma_start(q_t[:, :, 0:HALF], ctv[:, :, 0:HALF]).then_inc(ctxt_in[0], 16)
            load_wk(0)
            sp.dma_start(q_t[:, :, HALF:N], ctv[:, :, HALF:N]).then_inc(ctxt_in[1], 16)
            load_wv(0)
            for k in range(4):
                sp.dma_start(X[:, 2 * k:2 * k + 2, :], x[2 * k:2 * k + 2].rearrange("b t d -> t b d")).then_inc(x_in[k], 16)
            load_wq(0)
            load_wo(0)
            for g in range(1, KV):
                sp.wait_ge(kp_mm, CREDIT + 2 * g)
                load_wk(g)
                if g % 2 == 0:
                    sp.wait_ge(vp_mm, CREDIT + 2 * g)
                    load_wv(g // 2)
                sp.wait_ge(wo_lo_ok, CREDIT + G * g)
                load_wo(g)
                sp.wait_ge(qp_mm, CREDIT + 8 * g)
                load_wq(g)
            sp.wait_ge(qp_mm, CREDIT + 8 * KV)
            sp.dma_start(wb_raw[:, :, :], wbase_t.rearrange("(k p) n -> p k n", p=P)).then_inc(wb_in, 16)
            sp.dma_start(ar_raw[:, :, 0:P], lora_a_t.rearrange("(k p) n -> p k n", p=P)).then_inc(ar_in, 16)
            sp.dma_start(ar_raw[:, :, P:ZR], router_t.rearrange("(k p) n -> p k n", p=P)).then_inc(ar_in, 16)
            sp.dma_start(lb[:, :], lora_b).then_inc(lb_in, 16)
            sp.dma_start(bb[:, :], bbase.unsqueeze(0).to_broadcast([P, D])).then_inc(lb_in, 16)
            sp.wait_ge(x1_ok, CREDIT + B * KV)

            def load_ctx(b, j):
                sp.dma_start(ctx_s[:, j, :], ctx[b]).then_inc(ctxs_in[j], 16)

            load_ctx(0, 0)
            load_ctx(1, 1)
            for b in range(B):
                sp.dma_start(mask_bb[:, b, :], mask_b[b, 0:1, :].to_broadcast([P, D])).then_inc(maskb_in, 16)

            def load_expert(e, j):
                sp.dma_start(we_raw[:, j, :, :], we[e].rearrange("(k p) n -> p k n", p=P)).then_inc(we_in[j], 16)
                sp.dma_start(be_b[:, j, :], be[e].unsqueeze(0).to_broadcast([P, D])).then_inc(be_in[j], 16)

            sp.wait_ge(x2_ok, CREDIT + B)
            load_expert(0, 0)
            load_expert(1, 1)
            for b in range(2, B):
                sp.wait_ge(pq_mm, CREDIT + 5 * (b - 1))
                load_ctx(b, b % 2)
            for e in range(2, EX):
                sp.wait_ge(wel_ok, CREDIT + 4 * (e - 1))
                sp.wait_ge(td_ok, CREDIT + B * (e - 1))
                load_expert(e, e % 2)
            for b in range(B):
                sp.wait_ge(x4_ok, CREDIT + B * (EX - 1) + 1 + b)
                sp.dma_start(out[b], X[:, b, :]).then_inc(out_done, 16)
            sp.wait_ge(out_done, 16 * B)

        @block.gpsimd
        def _(gp):
            start_counts(gp, (ones_ok, eps_ok, rstd_ok, wkl_ok, wvl_ok, wql_ok, wo_lo_ok, rope_ok, wbl_ok, x2_ok, kz_ok,
                              va_ok, kb_ok, wel_ok))
            nc.gpsimd.memset(ln_eps[:, :], LN_EPS)
            nc.gpsimd.memset(minus_half[:, :], -0.5).then_inc(ones_ok, 1)
            nc.gpsimd.memset(ones[:, :], 1.0).then_inc(ones_ok, 1)
            nc.gpsimd.memset(v_ones[:, :, :, :], 1.0).then_inc(ones_ok, 1)

            def row_scale(n, b, j):
                gp.wait_ge(aggr_ok, CREDIT + B * n + b + 1)
                nc.gpsimd.tensor_tensor(var_eps[:, j:j + 1], mean_var[:, j, 1:2], ln_eps[:, :], ALU.add).then_inc(eps_ok, 1)
                nc.gpsimd.tensor_copy(mean[:, bass.ds(b, 1)], mean_var[:, j, 0:1])
                gp.wait_ge(eps_ok, CREDIT + B * n + b + 1)
                nc.gpsimd.tensor_tensor(rstd[:, bass.ds(b, 1)], var_eps[:, j:j + 1], minus_half[:, 0:1], ALU.pow).then_inc(rstd_ok, 1)

            def lo_part(dst, raw, hi, done):
                nc.gpsimd.tensor_tensor(dst, raw, hi.bitcast(F32), ALU.subtract).then_inc(done, 1)

            def wk_split(g):
                gp.wait_ge(wkh_ok, CREDIT + g + 1)
                lo_part(wk_lo[:, :, :], wk_raw[:, :, :], wk_hi[:, :, :], wkl_ok)

            def wv_split(p):
                gp.wait_ge(wvh_ok, CREDIT + p + 1)
                lo_part(wv_lo[:, :, :], wv_raw[:, :, :], wv_hi[:, :, :], wvl_ok)

            def wq_split(g, k):
                gp.wait_ge(wqh_ok, CREDIT + KT * g + k + 1)
                lo_part(wq_lo[:, k, :], wq_raw[:, k, :], wq_hi[:, k, :], wql_ok)

            def wo_split(g, k):
                gp.wait_ge(wo_hi_ok, CREDIT + G * g + k + 1)
                lo_part(wo_lo[:, k, :], wo_raw[:, k, :], wo_hi[:, k, :], wo_lo_ok)

            def rope_sum(g, r):
                gp.wait_ge(rot_ok, CREDIT + 10 * g + r + 1)
                if r < 2:
                    dst = k_t[:, r * HALF:(r + 1) * HALF]
                else:
                    half, head = divmod(r - 2, G)
                    dst = q_t[:, head, half * HALF:(half + 1) * HALF]
                nc.gpsimd.tensor_tensor(dst, rot_a[:, r % 2, :], rot_b[:, r % 2, :], ALU.add).then_inc(rope_ok, 1)

            def group(g, p, odd, last=False):
                for r in range(2, 10):
                    rope_sum(g, r)
                    if r < 2 + G:
                        wo_split(g, r - 2)
                if last:
                    for b in range(B):
                        row_scale(1, b, b % 2)
                        if b < KT:
                            gp.wait_ge(wbh_ok, CREDIT + b + 1)
                            lo_part(wb_lo[:, b, :], wb_raw[:, b, :], wb_hi[:, b, :], wbl_ok)
                        if b == KT:
                            gp.wait_ge(wbh_ok, CREDIT + KT + 1)
                            lo_part(ar_lo[:, :, :], ar_raw[:, :, :], ar_hi[:, :, :], wbl_ok)
                    return
                wk_split(g + 1)
                for k in range(KT):
                    wq_split(g + 1, k)
                if odd:
                    wv_split(p + 1)
                rope_sum(g + 1, 0)
                rope_sum(g + 1, 1)

            wk_split(0)
            rope_sum(0, 0)
            wv_split(0)
            rope_sum(0, 1)
            for b in range(B):
                row_scale(0, b, b % 2)
                if b >= KT:
                    wq_split(0, b - KT)
            with gp.Fori(0, PAIRS - 1) as p:
                group(2 * p, p, False)
                group(2 * p + 1, p, True)
            group(KV - 2, PAIRS - 1, False)
            group(KV - 1, PAIRS - 1, True, last=True)

            nc.gpsimd.memset(k_blk[:, :, :, :, :, :], 0.0).then_inc(kz_ok, 1)
            gp.wait_ge(x1_ok, CREDIT + B * KV)
            nc.gpsimd.memset(v_aug[:, :, :, :, :], 1.0).then_inc(va_ok, 1)

            def mixed(b, j):
                gp.wait_ge(tb_ok, CREDIT + b + 1)
                nc.gpsimd.tensor_tensor(X[:, b, :], X[:, b, :], t_b[:, j, :], ALU.add).then_inc(x2_ok, 1)

            mixed(0, 0)
            with gp.Fori(0, (B - 2) // 2) as i:
                mixed(2 * i + 1, 1)
                row_scale(2, 2 * i, 0)
                mixed(2 * i + 2, 0)
                row_scale(2, 2 * i + 1, 1)
            mixed(B - 1, 1)
            row_scale(2, B - 2, 0)
            row_scale(2, B - 1, 1)

            def keys(b, j):
                gp.wait_ge(mf_ok, CREDIT + b + 1)
                for grp in range(2):
                    gp.wait_ge(pq_ev, CREDIT + 4 * b + grp + 1)
                    for hd in range(4):
                        part = slice(32 * hd, 32 * hd + 32)
                        last = nc.gpsimd.tensor_tensor(
                            k_blk[part, j, grp, :, hd, :], heads(k_raw[part, grp, :]), heads(m_full[part, j, :]), ALU.mult)
                    last.then_inc(kb_ok, 1)

            gp.wait_ge(kz_ok, CREDIT + 1)
            gp.wait_ge(rstd_ok, CREDIT + 3 * B)
            with gp.Fori(0, B // 2) as i:
                for j in range(2):
                    keys(2 * i + j, j)

            def expert_lo(e, j, k):
                gp.wait_ge(weh_ok, CREDIT + 4 * e + k + 1)
                lo_part(we_lo[j][:, k, :], we_raw[:, j, k, :], we_hi[j][:, k, :], wel_ok)

            def attended(b, j):
                gp.wait_ge(tc_ok, CREDIT + b + 1)
                nc.gpsimd.tensor_tensor(X[:, b, :], X[:, b, :], t_c[:, j, :], ALU.add).then_inc(x3_ok, 1)

            for k in range(KT):
                expert_lo(0, 0, k)
            attended(0, 0)
            with gp.Fori(0, (B - 2) // 2) as i:
                attended(2 * i + 1, 1)
                row_scale(3, 2 * i, 0)
                attended(2 * i + 2, 0)
                row_scale(3, 2 * i + 1, 1)
            attended(B - 1, 1)
            row_scale(3, B - 2, 0)
            row_scale(3, B - 1, 1)
            with gp.Fori(0, EX // 2 - 1) as i:
                for k in range(KT):
                    expert_lo(2 * i + 1, 1, k)
                for k in range(KT):
                    expert_lo(2 * i + 2, 0, k)
            for k in range(KT):
                expert_lo(EX - 1, 1, k)

        @block.scalar
        def _(ac):
            small = [
                (ident[:, :], c_ident), (cos[:, :], c_cos), (sin[:, :], c_sin), (mask8[:, :], mask_tq),
                (gates[:, 0:2], g_xattn.unsqueeze(0).to_broadcast([P, 2])),
                (gates[:, 2:4], g_ffn.unsqueeze(0).to_broadcast([P, 2])),
                (iota[:, :], c_iota), (aug[:, :], c_aug), (lower[:, :, :], c_lower),
                (active_i[:, :], active.unsqueeze(0).to_broadcast([P, 4])),
                (prior_b[:, :], prior.unsqueeze(0).to_broadcast([P, ET])),
                (rb[:, :], router_b.unsqueeze(0).to_broadcast([P, ET])),
                (wq1[:, :, :], wq1p), (wk1[:, :, :], wk1p), (bq1[:, :], bq1p), (bk1[:, :], bk1p),
                (wv1[:, :], wv1t), (wo1[:, :], wo1t), (bv1_b[:, :], bv1.unsqueeze(0).to_broadcast([P, E1])),
                (bo1_c[:, :], bo1.unsqueeze(1)), (wg[:, :, :], wgate.rearrange("(k p) e -> p k e", p=P)),
                (bg[:, :], bgate.unsqueeze(0).to_broadcast([P, EX])),
            ]
            assert len(small) == N_SMALL
            for dst, src in small:
                ac.dma_start(dst, src).then_inc(consts_in, 16)
            start_counts(ac, (ot_ev, prep_a, gates_ok, hth_ok, cth_ok, wkh_ok, wvh_ok, wqh_ok, wo_hi_ok, v_ok, th_ok, ex_ok, ah_ok, wbh_ok,
                              lge_ok, zt_ok, pq_ev, p_ok, pt_ok, gelu_ok, weh_ok, r_ok))

            def hi_part(dst, raw, done):
                nc.scalar.activation(dst, raw, ACT.Copy).then_inc(done, 1)

            def wk_split(g):
                ac.wait_ge(wk_in, 16 * g + 16)
                hi_part(wk_hi[:, :, :], wk_raw[:, :, :], wkh_ok)

            def wv_split(p):
                ac.wait_ge(wv_in, 16 * p + 16)
                hi_part(wv_hi[:, :, :], wv_raw[:, :, :], wvh_ok)

            def wq_split(g, k):
                if k == 0:
                    ac.wait_ge(wq_in, 16 * g + 16)
                hi_part(wq_hi[:, k, :], wq_raw[:, k, :], wqh_ok)

            def wo_split(g, k):
                if k == 0:
                    ac.wait_ge(wo_in, 16 * g + 16)
                    ac.wait_ge(wo_mm, CREDIT + B * g)
                hi_part(wo_hi[:, k, :], wo_raw[:, k, :], wo_hi_ok)

            def values(p, t):
                ac.wait_ge(vp_mm, CREDIT + 4 * p + t + 1)
                nc.scalar.activation(v_ones[:, 2 * t:2 * t + 2, :, 0:P], ps[:, t % 2, :].rearrange("p (b s n) -> p b s n", b=2, s=2),
                                     ACT.Copy, scale=tanh_g[:, 0:1]).then_inc(v_ok, 1)

            for half in range(2):
                ac.wait_ge(ctxt_in[half], 16)
                cols = slice(half * HALF, (half + 1) * HALF)
                for k in range(KT):
                    hi_part(ct_hi[:, k, cols], q_t[:, k, cols], cth_ok)
                if half == 0:
                    wk_split(0)
            wv_split(0)
            ac.wait_ge(prep_v, CREDIT + 1)
            nc.scalar.activation(log_prior[:, :], prior_e[:, :], ACT.Ln).then_inc(prep_a, 1)
            nc.scalar.activation(tanh_g[:, :], gates[:, :], ACT.Tanh).then_inc(gates_ok, 1)
            ac.wait_ge(gates_ok, CREDIT + 1)
            ac.wait_ge(ones_ok, CREDIT + 3)
            for t in range(4):
                values(0, t)
            for b in range(B):
                ac.wait_ge(ht_mm, CREDIT + b + 1)
                nc.scalar.activation(xt_hi[:, :, b * P:(b + 1) * P], heads(ps[:, 4 + b % 2, :]), ACT.Copy).then_inc(hth_ok, 1)
                if b >= 3 and b < 3 + KT:
                    wq_split(0, b - 3)

            def group(g, p, odd, last=False, first=False):
                for k in range(G):
                    wo_split(g, k)
                if not odd and not first:
                    for t in range(4):
                        values(p, t)

                def weights(b):
                    bank = ps[:, 2 + b % 2, :]
                    ac.wait_ge(s_mm, CREDIT + B * g + b + 1)
                    nc.scalar.activation(bank, bank, ACT.Tanh, scale=LOGIT_SCALE / CAP).then_inc(th_ok, 1)
                    ac.wait_ge(th_ok, CREDIT + B * g + b + 1)
                    nc.scalar.activation(bank, bank, ACT.Exp, scale=CAP).then_inc(ex_ok, 1)

                weights(0)
                weights(1)
                for b in range(B):
                    if b + 2 < B:
                        weights(b + 2)
                    ac.wait_ge(at_mm, CREDIT + B * g + b + 1)
                    ac.wait_ge(wo_mm, CREDIT + B * g + b - 1)
                    nc.scalar.activation(at_hi[:, b % 2, :], ps[:, 6, :], ACT.Copy).then_inc(ah_ok, 1)
                    if last:
                        if b == 0:
                            ac.wait_ge(wb_in, 16)
                        if b < KT:
                            hi_part(wb_hi[:, b, :], wb_raw[:, b, :], wbh_ok)
                        if b == KT:
                            ac.wait_ge(ar_in, 32)
                            hi_part(ar_hi[:, :, :], ar_raw[:, :, :], wbh_ok)
                    elif b == 0:
                        wk_split(g + 1)
                    elif b < 1 + KT:
                        wq_split(g + 1, b - 1)
                    elif b == 1 + KT and odd:
                        wv_split(p + 1)

            group(0, 0, False, first=True)
            group(1, 0, True)
            with ac.Fori(1, PAIRS - 1) as p:
                group(2 * p, p, False)
                group(2 * p + 1, p, True)
            group(KV - 2, PAIRS - 1, False)
            group(KV - 1, PAIRS - 1, True, last=True)

            def row_hi(b, j):
                ac.wait_ge(ht_mm, CREDIT + B + b + 1)
                ac.wait_ge(yb_mm, CREDIT + b - 1)
                nc.scalar.activation(ht_hi[:, j, :], ps[:, j, :], ACT.Copy).then_inc(hth_ok, 1)

            def mix(b, j, more):
                if more:
                    row_hi(b + 1, 1 - j)
                ac.wait_ge(lgm_ok, CREDIT + b + 1)
                nc.scalar.activation(lg_e[:, j, :], lg[:, j, :], ACT.Exp, bias=lg_max[:, j:j + 1]).then_inc(lge_ok, 1)
                ac.wait_ge(zt_mm, CREDIT + b + 1)
                nc.scalar.activation(z_wt[:, j, :], ps[:, 6, 0:P], ACT.Copy).then_inc(zt_ok, 1)

            ac.wait_ge(ht_mm, CREDIT + B + 1)
            nc.scalar.activation(ht_hi[:, 0, :], ps[:, 0, :], ACT.Copy).then_inc(hth_ok, 1)
            with ac.Fori(0, B // 2 - 1) as i:
                for j in range(2):
                    mix(2 * i + j, j, True)
            mix(B - 2, 0, True)
            mix(B - 1, 1, False)

            def proj_out(b, j, n):
                dst, bias = ((k_raw[:, 0, :], bk1a[:, 0:1]), (k_raw[:, 1, :], bk1a[:, 1:2]),
                             (q_pad[:, j, 0, :], bq1a[:, 0:1]), (q_pad[:, j, 1, :], bq1a[:, 1:2]))[n]
                ac.wait_ge(pq_mm, CREDIT + 5 * b + n + 1)
                if n < 2:
                    ac.wait_ge(kb_ok, CREDIT + 2 * b - 1 + n)
                nc.scalar.activation(dst, ps[:, n % 2, :], ACT.Identity, bias=bias).then_inc(pq_ev, 1)

            def turned(b, u):
                ac.wait_ge(pt_mm, CREDIT + 8 * b + u + 1)
                ac.wait_ge(pv2_mm, CREDIT + 8 * b + u - 1)
                nc.scalar.activation(p_t[:, u % 2, :], ps[:, 4 + u % 2, :], ACT.Copy).then_inc(pt_ok, 1)

            def out_turned(b, j):
                ac.wait_ge(ot_mm, CREDIT + b + 1)
                nc.scalar.activation(o_t[:, b, :], ps[0:E1, 6 + j, :], ACT.Copy).then_inc(ot_ev, 1)

            def batch(b, j, first=False, last=False):
                for u in range(H1):
                    ac.wait_ge(sb_ok, CREDIT + 8 * b + u + 1)
                    ac.wait_ge(pt_mm, CREDIT + 8 * b + u - 1)
                    nc.scalar.activation(p_w[:, u % 2, :], s_sub[:, u % 2, :], ACT.Exp, scale=INV_SQRT_DH).then_inc(p_ok, 1)
                    if u >= 1:
                        turned(b, u - 1)
                    elif not first:
                        turned(b - 1, H1 - 1)
                    if u == 4 and not first:
                        out_turned(b - 1, 1 - j)
                    if not last and 2 <= u <= 5:
                        proj_out(b + 1, 1 - j, u - 2)

            for n in range(4):
                proj_out(0, 0, n)
            batch(0, 0, first=True)
            with ac.Fori(0, (B - 2) // 2) as i:
                batch(2 * i + 1, 1)
                batch(2 * i + 2, 0)
            batch(B - 1, 1, last=True)
            turned(B - 1, H1 - 1)
            out_turned(B - 1, 1)
            ac.wait_ge(ot_ev, CREDIT + B)

            def expert_hi(e, j, k):
                if k == 0:
                    ac.wait_ge(we_in[j], 8 * (e - j) + 16)
                    ac.wait_ge(y2_mm, CREDIT + B * (e - 1))
                hi_part(we_hi[j][:, k, :], we_raw[:, j, k, :], weh_ok)

            for b in range(B):
                nc.scalar.activation(o_t[:, b, :], o_t[:, b, :], ACT.Gelu).then_inc(gelu_ok, 1)
                if b == 1:
                    ac.wait_ge(we_in[0], 16)
                if 1 <= b < 1 + KT:
                    hi_part(we_hi[0][:, b - 1, :], we_raw[:, 0, b - 1, :], weh_ok)
            with ac.Fori(0, B // 2) as i:
                for j in range(2):
                    ac.wait_ge(ht_mm, CREDIT + 2 * B + 2 * i + j + 1)
                    nc.scalar.activation(xt_hi[:, :, bass.ds((2 * i + j) * P, P)], heads(ps[:, j, :]), ACT.Copy).then_inc(hth_ok, 1)

            def expert(e, j, more):
                for b in range(B):
                    if more and b < KT:
                        expert_hi(e + 1, 1 - j, b)
                    if b == 0:
                        ac.wait_ge(sel_ok, CREDIT + 1)
                    ac.wait_ge(td_ok, CREDIT + B * e + b + 1)
                    ac.wait_ge(x4_ok, CREDIT + B * e + b - 1)
                    nc.scalar.activation(r_d[:, b % 2, :], t_d[:, b % 2, :], ACT.Relu, scale=sel[:, b, bass.ds(e, 1)]).then_inc(r_ok, 1)

            with ac.Fori(0, EX // 2 - 1) as i:
                for j in range(2):
                    expert(2 * i + j, j, True)
            expert(EX - 2, 0, True)
            expert(EX - 1, 1, False)

        @block.vector
        def _(ve):
            start_counts(ve, (wo1_ok, ctl_ok, prep_v, cap_ok, stat_ok, aggr_ok, h_ok, htl_ok, rot_ok, e_ok, rec_ok, at_ok, al_ok,
                              x1_ok, bbg_ok, lg_ok, lgm_ok, lgs_ok, lgi_ok, al2_ok, zw_ok, tb_ok, hc_ok, mm_ok, mf_ok,
                              cv_ok, mx_ok, sb_ok, oi_ok, on_ok, tc_ok, x3_ok, sel_ok, rank_ok, td_ok, x4_ok))
            def row_stats(n, b, j, ready, before=0):
                ve.wait_ge(ready, 16 if n == 0 else CREDIT + before + b + 1)
                nc.vector.bn_stats(stats[:, j, :], X[:, b, :]).then_inc(stat_ok, 1)
                ve.wait_ge(stat_ok, CREDIT + B * n + b + 1)
                ve.wait_ge(rstd_ok, CREDIT + B * n + b - 1)
                nc.vector.bn_aggr(mean_var[:, j, :], stats[:, j, :]).then_inc(aggr_ok, 1)

            def normalise(b, j, done):
                nc.vector.tensor_scalar(h[:, j, :], X[:, b, :], mean[:, bass.ds(b, 1)], rstd[:, bass.ds(b, 1)],
                                        ALU.subtract, ALU.mult).then_inc(done, 1)

            for half in range(2):
                cols = slice(half * HALF, (half + 1) * HALF)
                for k in range(KT):
                    ve.wait_ge(cth_ok, CREDIT + KT * half + k + 1)
                    nc.vector.tensor_tensor(ct_lo[:, k, cols], q_t[:, k, cols], ct_hi[:, k, cols].bitcast(F32), ALU.subtract).then_inc(ctl_ok, 1)

            ve.wait_ge(consts_in, 16 * N_SMALL)
            nc.vector.tensor_scalar(prior_e[:, :], prior_b[:, :], 1e-12, None, ALU.add).then_inc(prep_v, 1)
            nc.vector.tensor_copy(active_f[:, :], active_i[:, :]).then_inc(prep_v, 1)
            nc.vector.tensor_copy(maskf[:, :], mask8[:, :]).then_inc(prep_v, 1)
            nc.vector.tensor_copy(wg_hi[:, :, :], wg[:, :, :]).then_inc(prep_v, 1)
            nc.vector.memset(count[:, 0, :], 0.0).then_inc(prep_v, 1)
            nc.vector.tensor_scalar(bq1a[:, :], bq1[:, :], aug[:, 2:3], None, ALU.add).then_inc(prep_v, 1)
            nc.vector.tensor_scalar(bk1a[:, :], bk1[:, :], aug[:, 2:3], None, ALU.add).then_inc(prep_v, 1)
            step = 7
            ve.wait_ge(prep_v, CREDIT + step)
            nc.vector.tensor_tensor(wg_lo[:, :, :], wg[:, :, :], wg_hi[:, :, :].bitcast(F32), ALU.subtract).then_inc(prep_v, 1)
            for k in range(4):
                nc.vector.scalar_tensor_tensor(count[:, k + 1, :], iota[:, :], active_f[:, k:k + 1], count[:, k, :],
                                               ALU.is_equal, ALU.add).then_inc(prep_v, 1)
                ve.wait_ge(prep_v, CREDIT + step + k + 2)
            step += 5
            nc.vector.tensor_scalar(absent[:, :], count[:, 4, :], 0.5, BIG, ALU.is_gt, ALU.mult).then_inc(prep_v, 1)
            def rotate(g, r):
                bank = ps[:, r % 2, :]
                if r < 2:
                    ve.wait_ge(kp_mm, CREDIT + 2 * g + r + 1)
                else:
                    ve.wait_ge(qp_mm, CREDIT + 8 * g + r - 1)
                ve.wait_ge(rope_ok, CREDIT + 10 * g + r - 1)
                nc.vector.tensor_tensor(heads(rot_a[:, r % 2, :]), heads(bank), bcast(cos[:, :], 4), ALU.mult)
                nc.vector.tensor_tensor(heads(rot_b[0:64, r % 2, :]), heads(bank[64:128, :]), bcast(sin[64:128, :], 4), ALU.mult)
                nc.vector.tensor_tensor(heads(rot_b[64:128, r % 2, :]), heads(bank[0:64, :]), bcast(sin[0:64, :], 4),
                                        ALU.mult).then_inc(rot_ok, 1)

            def turned(n, b, bank):
                ve.wait_ge(hth_ok, CREDIT + B * n + b + 1)
                nc.vector.tensor_tensor(xt_lo[:, :, b * P:(b + 1) * P], heads(ps[:, bank, :]),
                                        xt_hi[:, :, b * P:(b + 1) * P].bitcast(F32), ALU.subtract).then_inc(htl_ok, 1)

            rotate(0, 0)
            rotate(0, 1)
            for b in range(B + 3):
                if b < B:
                    row_stats(0, b, b % 2, x_in[b // 2])
                if 2 <= b < B + 2:
                    ve.wait_ge(rstd_ok, CREDIT + b - 1)
                    normalise(b - 2, b % 2, h_ok)
                if b >= 3:
                    turned(0, b - 3, 4 + (b - 3) % 2)
            ve.wait_ge(prep_a, CREDIT + 1)
            nc.vector.tensor_tensor(route_1[:, :], log_prior[:, :], rb[:, :], ALU.add).then_inc(prep_v, 1)
            ve.wait_ge(prep_v, CREDIT + step + 2)
            nc.vector.tensor_scalar(absent2[:, :], absent[:, :], -BIG, None, ALU.add).then_inc(prep_v, 1)
            ve.wait_ge(prep_v, CREDIT + step + 3)
            nc.vector.tensor_tensor(route_bias[:, :], route_1[:, :], absent2[:, :], ALU.add).then_inc(prep_v, 1)
            ve.wait_ge(prep_mm, CREDIT + 1)
            nc.vector.tensor_scalar(cap[:, :], ps[:, 7, 0:P], 0.5, TINY, ALU.is_lt, ALU.mult).then_inc(prep_v, 1)
            ve.wait_ge(prep_v, CREDIT + step + 5)
            nc.vector.scalar_tensor_tensor(cap[:, :], maskf[:, :], BIG, cap[:, :], ALU.mult, ALU.add).then_inc(cap_ok, 1)

            ve.wait_ge(cap_ok, CREDIT + 1)

            def group(g, last=False):
                def mask(b):
                    ve.wait_ge(ex_ok, CREDIT + B * g + b + 1)
                    ve.wait_ge(pv_mm, CREDIT + B * g + b - 1)
                    nc.vector.tensor_tensor(heads(e_w[:, b % 2, :]), heads(ps[:, 2 + b % 2, :]), bcast(cap[:, :], G),
                                            ALU.min).then_inc(e_ok, 1)

                def scale(b):
                    o = ps[:, 4:6, 0:2 * (P + 1)].rearrange("p a (c n) -> p a c n", c=2)
                    inv = denom_inv[:, b % 2, :].rearrange("p (a c) -> p a c", a=2)
                    ve.wait_ge(pv_mm, CREDIT + B * g + b + 1)
                    nc.vector.reciprocal(inv, o[:, :, :, P]).then_inc(rec_ok, 1)
                    ve.wait_ge(rec_ok, CREDIT + B * g + b + 1)
                    ve.wait_ge(at_mm, CREDIT + B * g + b - 1)
                    nc.vector.tensor_tensor(attn[:, b % 2, :].rearrange("p (a c n) -> p a c n", a=2, c=2), o[:, :, :, 0:P],
                                            inv.unsqueeze(3).to_broadcast([P, 2, 2, P]), ALU.mult).then_inc(at_ok, 1)

                def lo_of(b):
                    ve.wait_ge(ah_ok, CREDIT + B * g + b + 1)
                    ve.wait_ge(wo_mm, CREDIT + B * g + b - 1)
                    nc.vector.tensor_tensor(at_lo[:, b % 2, :], ps[:, 6, :], at_hi[:, b % 2, :].bitcast(F32),
                                            ALU.subtract).then_inc(al_ok, 1)

                def add(b):
                    ve.wait_ge(wo_mm, CREDIT + B * g + b + 1)
                    nc.vector.tensor_tensor(X[:, b, :], ps[:, 7, :], X[:, b, :], ALU.add).then_inc(x1_ok, 1)
                    if last and b >= 1:
                        row_stats(1, b - 1, (b - 1) % 2, x1_ok, B * LAST)

                for r in range(2, 8):
                    rotate(g, r)
                mask(0)
                mask(1)
                rotate(g, 8)
                scale(0)
                mask(2)
                rotate(g, 9)
                lo_of(0)
                for b in range(1, B):
                    scale(b)
                    if b + 2 < B:
                        mask(b + 2)
                    add(b - 1)
                    if b == B - 1 and not last:
                        rotate(g + 1, 0)
                    lo_of(b)
                if not last:
                    rotate(g + 1, 1)
                add(B - 1)

            with ve.Fori(0, LAST) as g:
                group(g)
            group(LAST, last=True)

            ve.wait_ge(lb_in, 32)
            ve.wait_ge(gates_ok, CREDIT + 1)
            nc.vector.tensor_scalar(bbg[:, :], bb[:, :], tanh_g[:, 2:3], None, ALU.mult).then_inc(bbg_ok, 1)
            row_stats(1, B - 1, 1, x1_ok, B * LAST)
            ve.wait_ge(bbg_ok, CREDIT + 1)

            def mix_lo(b, j):
                ve.wait_ge(hth_ok, CREDIT + B + b + 1)
                nc.vector.tensor_tensor(ht_lo[:, j, :], ps[:, j, :], ht_hi[:, j, :].bitcast(F32), ALU.subtract).then_inc(htl_ok, 1)

            def mixed(b, j):
                ve.wait_ge(y_mm, CREDIT + b + 1)
                ve.wait_ge(x2_ok, CREDIT + b - 1)
                nc.vector.scalar_tensor_tensor(t_b[:, j, :], ps[:, 4 + j, :], tanh_g[:, 2:3], bbg[:, :], ALU.mult, ALU.add).then_inc(tb_ok, 1)

            def mix(b, j, first=False, last=False):
                ve.wait_ge(z_mm, CREDIT + b + 1)
                nc.vector.tensor_tensor(lg[:, j, :], ps[:, 2 + j, P:ZR], route_bias[:, :], ALU.add).then_inc(lg_ok, 1)
                ve.wait_ge(lg_ok, CREDIT + b + 1)
                nc.vector.tensor_reduce(lg_max[:, j:j + 1], lg[:, j, :], AX.X, ALU.max, negate=True).then_inc(lgm_ok, 1)
                if not last:
                    mix_lo(b + 1, 1 - j)
                ve.wait_ge(lge_ok, CREDIT + b + 1)
                nc.vector.tensor_tensor_reduce(out=lg_n[:, j, :], in0=lg_e[:, j, :], in1=count[:, 4, :], scale=1.0, scalar=0.0,
                                               op0=ALU.mult, op1=ALU.add, accum_out=lg_sum[:, j:j + 1]).then_inc(lgs_ok, 1)
                ve.wait_ge(lgs_ok, CREDIT + b + 1)
                nc.vector.reciprocal(lg_inv[:, j:j + 1], lg_sum[:, j:j + 1]).then_inc(lgi_ok, 1)
                ve.wait_ge(lgi_ok, CREDIT + b + 1)
                nc.vector.tensor_scalar(alpha[:, j, :], lg_n[:, j, :], lg_inv[:, j:j + 1], 2.0, ALU.mult, ALU.mult).then_inc(al2_ok, 1)
                ve.wait_ge(al2_ok, CREDIT + b + 1)
                nc.vector.tensor_tensor(z_w[:, j, :].rearrange("p (e r) -> p e r", e=ET),
                                        ps[:, 2 + j, 0:P].rearrange("p (e r) -> p e r", e=ET),
                                        alpha[:, j, :].unsqueeze(2).to_broadcast([P, ET, RANK]), ALU.mult).then_inc(zw_ok, 1)
                if b + 2 < B:
                    first_rows(b + 2, j)
                if not first:
                    mixed(b - 1, 1 - j)

            def first_rows(b, j):
                ve.wait_ge(rstd_ok, CREDIT + B + b + 1)
                normalise(b, j, h_ok)

            first_rows(0, 0)
            first_rows(1, 1)
            mix_lo(0, 0)
            mix(0, 0, first=True)
            mix(1, 1)
            for b in range(2, B):
                mix(b, b % 2, last=b == B - 1)
                row_stats(2, b - 2, b % 2, x2_ok)

            def rows(b, j):
                ve.wait_ge(rstd_ok, CREDIT + B * 2 + b + 1)
                normalise(b, j, hc_ok)
                nc.vector.tensor_scalar(m_mul[:, j, :], mask_bb[:, b, :], 0.0, aug[:, 0:1], ALU.is_gt, ALU.mult).then_inc(mm_ok, 1)

            def factors(b, j):
                ve.wait_ge(mm_ok, CREDIT + b + 1)
                nc.vector.tensor_scalar(m_full[:, j, :], m_mul[:, j, :], aug[:, 1:2], None, ALU.add).then_inc(mf_ok, 1)

            def values(b, j):
                ve.wait_ge(pq_mm, CREDIT + 5 * b + 5)
                nc.vector.tensor_tensor(v_aug[:, j, :, :, 0:DH],
                                        ps[:, 0, 0:PATCH * E1].rearrange("p (a h d) -> p a h d", a=PATCH, h=H1),
                                        bv1_b[:, :].rearrange("p (h d) -> p h d", h=H1).unsqueeze(1).to_broadcast([P, PATCH, H1, DH]),
                                        ALU.add).then_inc(cv_ok, 1)

            def row_max(b, u):
                ve.wait_ge(s2_mm, CREDIT + 8 * b + u + 1)
                nc.vector.tensor_reduce(s_max[:, u % 2, :], heads(ps[:, 2 + u % 2, :]), AX.X, ALU.max).then_inc(mx_ok, 1)

            def less_max(b, u):
                ve.wait_ge(mx_ok, CREDIT + 8 * b + u + 1)
                ve.wait_ge(p_ok, CREDIT + 8 * b + u - 1)
                nc.vector.tensor_tensor(heads(s_sub[:, u % 2, :]), heads(ps[:, 2 + u % 2, :]),
                                        s_max[:, u % 2, :].unsqueeze(2).to_broadcast([P, 4, P]), ALU.subtract).then_inc(sb_ok, 1)

            def over_sums(b, j):
                o = ps[:, 6 + j, 0:PATCH * H1 * VA].rearrange("p (a n) -> p a n", n=VA)
                ve.wait_ge(pv2_mm, CREDIT + 8 * b + 8)
                nc.vector.reciprocal(o_inv[:, j, :], o[:, :, DH]).then_inc(oi_ok, 1)
                ve.wait_ge(oi_ok, CREDIT + b + 1)
                nc.vector.tensor_tensor(o_n[:, j, :].rearrange("p (a d) -> p a d", d=DH), o[:, :, 0:DH],
                                        o_inv[:, j, :].unsqueeze(2).to_broadcast([P, PATCH * H1, DH]), ALU.mult).then_inc(on_ok, 1)

            def batch(b, j, first=False, last=False):
                for u in range(H1):
                    row_max(b, u)
                    less_max(b, u)
                    if u == 0 and not last:
                        rows(b + 1, 1 - j)
                    if u == 1 and not last:
                        factors(b + 1, 1 - j)
                    if u == 2 and not first:
                        over_sums(b - 1, 1 - j)
                    if u == 6 and not last:
                        values(b + 1, 1 - j)

            ve.wait_ge(maskb_in, 16 * B)
            rows(0, 0)
            factors(0, 0)
            mixed(B - 1, 1)
            row_stats(2, B - 2, 0, x2_ok)
            row_stats(2, B - 1, 1, x2_ok)
            ve.wait_ge(va_ok, CREDIT + 1)
            values(0, 0)
            nc.vector.tensor_scalar(wo1g[:, :], wo1[:, :], tanh_g[0:E1, 1:2], None, ALU.mult).then_inc(wo1_ok, 1)
            nc.vector.tensor_scalar(bo1g[:, :], bo1_c[:, :], tanh_g[:, 1:2], None, ALU.mult).then_inc(wo1_ok, 1)
            batch(0, 0, first=True)
            with ve.Fori(0, (B - 2) // 2) as i:
                batch(2 * i + 1, 1)
                batch(2 * i + 2, 0)
            batch(B - 1, 1, last=True)
            over_sums(B - 1, 1)

            ve.wait_ge(wo1_ok, CREDIT + 2)

            def output(b, j):
                ve.wait_ge(c2_mm, CREDIT + b + 1)
                ve.wait_ge(x3_ok, CREDIT + b - 1)
                nc.vector.scalar_tensor_tensor(t_c[:, j, :], ps[:, 2 + j, :], bo1g[:, 0:1], mask_bb[:, b, :],
                                               ALU.add, ALU.mult).then_inc(tc_ok, 1)

            def final_rows(b, j):
                ve.wait_ge(rstd_ok, CREDIT + B * 3 + b + 1)
                normalise(b, j, h_ok)

            output(0, 0)
            output(1, 1)
            row_stats(3, 0, 0, x3_ok)
            output(2, 0)
            row_stats(3, 1, 1, x3_ok)
            final_rows(0, 0)
            for b in range(3, B + 3):
                if b < B:
                    output(b, b % 2)
                if b - 1 < B:
                    row_stats(3, b - 1, (b - 1) % 2, x3_ok)
                if b - 2 < B:
                    final_rows(b - 2, b % 2)
                turned(2, b - 3, (b - 3) % 2)

            ve.wait_ge(gate_mm, CREDIT + B)
            nc.vector.tensor_tensor(gl[:, :, :], ps[:, 3, 0:B * EX].rearrange("p (b e) -> p b e", b=B), bcast(bg[:, :], B), ALU.add).then_inc(rank_ok, 1)
            ve.wait_ge(rank_ok, CREDIT + 1)
            other = gl[:, :, :].unsqueeze(2).to_broadcast([P, B, EX, EX])
            mine = gl[:, :, :].unsqueeze(3).to_broadcast([P, B, EX, EX])
            nc.vector.tensor_tensor(rank_a[:, :, :, :], other, mine, ALU.is_gt).then_inc(rank_ok, 1)
            nc.vector.tensor_tensor(rank_b[:, :, :, :], other, mine, ALU.is_equal).then_inc(rank_ok, 1)
            ve.wait_ge(rank_ok, CREDIT + 3)
            nc.vector.tensor_tensor(rank_b[:, :, :, :], rank_b[:, :, :, :], lower[:, :, :].unsqueeze(1).to_broadcast([P, B, EX, EX]), ALU.mult).then_inc(rank_ok, 1)
            ve.wait_ge(rank_ok, CREDIT + 4)
            nc.vector.tensor_tensor(rank_a[:, :, :, :], rank_a[:, :, :, :], rank_b[:, :, :, :], ALU.add).then_inc(rank_ok, 1)
            ve.wait_ge(rank_ok, CREDIT + 5)
            nc.vector.tensor_reduce(rank[:, :, :], rank_a[:, :, :, :], AX.X, ALU.add).then_inc(rank_ok, 1)
            ve.wait_ge(rank_ok, CREDIT + 6)
            nc.vector.tensor_scalar(sel[:, :, :], rank[:, :, :], 1.5, 0.5, ALU.is_lt, ALU.mult).then_inc(sel_ok, 1)

            def expert(e, j):
                ve.wait_ge(be_in[j], 8 * (e - j) + 16)

                def update(b):
                    ve.wait_ge(r_ok, CREDIT + B * e + b + 1)
                    nc.vector.scalar_tensor_tensor(X[:, b, :], r_d[:, b % 2, :], tanh_g[:, 3:4], X[:, b, :],
                                                   ALU.mult, ALU.add).then_inc(x4_ok, 1)

                for b in range(B):
                    ve.wait_ge(y2_mm, CREDIT + B * e + b + 1)
                    ve.wait_ge(r_ok, CREDIT + B * e + b - 1)
                    nc.vector.tensor_tensor(t_d[:, b % 2, :], ps[:, 4 + b % 4, :], be_b[:, j, :], ALU.add).then_inc(td_ok, 1)
                    if b >= 1:
                        update(b - 1)
                update(B - 1)

            with ve.Fori(0, EX // 2) as i:
                for j in range(2):
                    expert(2 * i + j, j)

        @block.tensor
        def _(pe):
            start_counts(pe, (ot_mm, prep_mm, ht_mm, kp_mm, vp_mm, qp_mm, yb_mm, s_mm, pv_mm, at_mm, wo_mm, z_mm, zt_mm, y_mm, pq_mm, s2_mm,
                              pt_mm, pv2_mm, c2_mm, gate_mm, y2_mm))
            def product(dst, pairs, start=True, stop=True):
                n = len(pairs)
                for k, (w_hi, w_lo, x_hi, x_lo) in enumerate(pairs):
                    nc.tensor.matmul(dst, w_hi, x_hi, start=start and k == 0, stop=False)
                    nc.tensor.matmul(dst, w_hi, x_lo, start=False, stop=False)
                    last = nc.tensor.matmul(dst, w_lo, x_hi, start=False, stop=stop and k == n - 1)
                return last

            def turn_rows(n, b, j, bank):
                pe.wait_ge(h_ok, CREDIT + B * n + b + 1)
                pe.wait_ge(htl_ok, CREDIT + B * n + b - 1)
                for k in range(KT):
                    last = nc.tensor.transpose(ps[:, bank, k * P:(k + 1) * P], h[:, j, k * P:(k + 1) * P], ident[:, :])
                last.then_inc(ht_mm, 1)

            def key_tile(g, half):
                if half == 0:
                    pe.wait_ge(wkl_ok, CREDIT + g + 1)
                cols = slice(half * HALF, (half + 1) * HALF)
                product(ps[:, half, :], [(wk_hi[:, k, :], wk_lo[:, k, :], ct_hi[:, k, cols], ct_lo[:, k, cols])
                                         for k in range(KT)]).then_inc(kp_mm, 1)

            def value_tile(p, t):
                if t == 0:
                    pe.wait_ge(wvl_ok, CREDIT + p + 1)
                if t < 2:
                    pe.wait_ge(rot_ok, CREDIT + 20 * p + t + 1)
                else:
                    pe.wait_ge(v_ok, CREDIT + 4 * p + t - 1)
                for c in range(2):
                    rows = slice((2 * t + c) * P, (2 * t + c + 1) * P)
                    last = product(ps[:, t % 2, c * 2 * P:(c + 1) * 2 * P],
                                   [(ct_hi[:, k, rows], ct_lo[:, k, rows], wv_hi[:, k, :], wv_lo[:, k, :]) for k in range(KT)])
                last.then_inc(vp_mm, 1)

            for half in range(2):
                pe.wait_ge(ctl_ok, CREDIT + KT * (half + 1))
                key_tile(0, half)
            pe.wait_ge(ones_ok, CREDIT + 2)
            pe.wait_ge(prep_v, CREDIT + 3)
            pe.wait_ge(consts_in, 16 * N_SMALL)
            nc.tensor.matmul(ps[:, 7, 0:P], ones[:, :], maskf[:, :], start=True, stop=True).then_inc(prep_mm, 1)
            for t in range(4):
                value_tile(0, t)
            for b in range(B):
                turn_rows(0, b, b % 2, 4 + b % 2)
            pe.wait_ge(cap_ok, CREDIT + 1)
            pe.wait_ge(ones_ok, CREDIT + 3)

            def group(g, p, odd, last=False, first=False):
                def query_tile(q):
                    half, head = divmod(q, G)
                    cols, rows = slice(half * HALF, (half + 1) * HALF), slice(head * P, (head + 1) * P)
                    if q == 0:
                        pe.wait_ge(wql_ok, CREDIT + KT * (g + 1))
                    if first and head == 0:
                        pe.wait_ge(htl_ok, CREDIT + 4 * half + 4)
                    if q >= 2:
                        pe.wait_ge(rot_ok, CREDIT + 10 * g + q + 1)
                    elif odd:
                        pe.wait_ge(rot_ok, CREDIT + 10 * g + q + 1)
                    else:
                        pe.wait_ge(v_ok, CREDIT + 4 * p + q + 3)
                    product(ps[:, q % 2, :], [(wq_hi[:, k, rows], wq_lo[:, k, rows], xt_hi[:, k, cols], xt_lo[:, k, cols])
                                              for k in range(KT)]).then_inc(qp_mm, 1)

                def next_keys(half):
                    if not last:
                        pe.wait_ge(rot_ok, CREDIT + 10 * g + 9 + half)
                        key_tile(g + 1, half)

                def scores(b):
                    if b in (0, 4):
                        pe.wait_ge(rope_ok, CREDIT + 10 * g + 6 + b)
                    pe.wait_ge(e_ok, CREDIT + B * g + b - 1)
                    nc.tensor.matmul(ps[:, 2 + b % 2, :], k_t[:, b * P:(b + 1) * P], q_t[:, :, b * P:(b + 1) * P],
                                     start=True, stop=True).then_inc(s_mm, 1)

                def weighted(b):
                    pe.wait_ge(e_ok, CREDIT + B * g + b + 1)
                    pe.wait_ge(at_ok, CREDIT + B * g + b)
                    for n in range(G):
                        at = (n % 2) * (P + 1)
                        last = nc.tensor.matmul(ps[:, 4 + n // 2, at:at + P + 1], e_w[:, b % 2, n * P:(n + 1) * P],
                                                v_ones[:, b, 1 if odd else 0, 0:P + 1], start=True, stop=True)
                    last.then_inc(pv_mm, 1)

                def turn(b):
                    pe.wait_ge(at_ok, CREDIT + B * g + b + 1)
                    pe.wait_ge(al_ok, CREDIT + B * g + b)
                    for n in range(G):
                        last = nc.tensor.transpose(ps[:, 6, n * P:(n + 1) * P], attn[:, b % 2, n * P:(n + 1) * P], ident[:, :])
                    last.then_inc(at_mm, 1)

                def output(b):
                    if b == 0:
                        pe.wait_ge(wo_lo_ok, CREDIT + G * (g + 1))
                    pe.wait_ge(al_ok, CREDIT + B * g + b + 1)
                    pe.wait_ge(x1_ok, CREDIT + B * g + b)
                    product(ps[:, 7, :], [(at_hi[:, b % 2, n * P:(n + 1) * P], at_lo[:, b % 2, n * P:(n + 1) * P],
                                           wo_hi[:, n, :], wo_lo[:, n, :]) for n in range(G)]).then_inc(wo_mm, 1)

                if not odd and not first:
                    for t in range(4):
                        value_tile(p, t)
                for q in range(6):
                    query_tile(q)
                scores(0)
                scores(1)
                query_tile(6)
                weighted(0)
                scores(2)
                query_tile(7)
                turn(0)
                for b in range(1, B):
                    weighted(b)
                    if b + 2 < B:
                        scores(b + 2)
                    output(b - 1)
                    if b == B - 1:
                        next_keys(0)
                    turn(b)
                next_keys(1)
                output(B - 1)

            group(0, 0, False, first=True)
            group(1, 0, True)
            with pe.Fori(1, PAIRS - 1) as p:
                group(2 * p, p, False)
                group(2 * p + 1, p, True)
            group(KV - 2, PAIRS - 1, False)
            group(KV - 1, PAIRS - 1, True, last=True)

            pe.wait_ge(wbl_ok, CREDIT + KT + 1)
            pe.wait_ge(lb_in, 32)

            def lora(b, j):
                pe.wait_ge(zw_ok, CREDIT + b + 1)
                pe.wait_ge(zt_ok, CREDIT + b)
                nc.tensor.transpose(ps[:, 6, 0:P], z_w[:, j, :], ident[:, :]).then_inc(zt_mm, 1)

            def lora_out(b, j):
                pe.wait_ge(zt_ok, CREDIT + b + 1)
                nc.tensor.matmul(ps[:, 4 + j, :], z_wt[:, j, :], lb[:, :], start=False, stop=True).then_inc(y_mm, 1)

            def mix(b, j, first=False, last=False):
                if not last:
                    turn_rows(1, b + 1, 1 - j, 1 - j)
                pe.wait_ge(htl_ok, CREDIT + B + b + 1)
                pe.wait_ge(zw_ok, CREDIT + b - 1)
                rows = [(ht_hi[:, j, k * P:(k + 1) * P], ht_lo[:, j, k * P:(k + 1) * P]) for k in range(KT)]
                product(ps[:, 2 + j, 0:ZR], [(*rows[k], ar_hi[:, k, :], ar_lo[:, k, :]) for k in range(KT)]).then_inc(z_mm, 1)
                if not first:
                    lora(b - 1, 1 - j)
                pe.wait_ge(tb_ok, CREDIT + b - 1)
                product(ps[:, 4 + j, :], [(*rows[k], wb_hi[:, k, :], wb_lo[:, k, :]) for k in range(KT)], stop=False).then_inc(yb_mm, 1)
                if not first:
                    lora_out(b - 1, 1 - j)

            turn_rows(1, 0, 0, 0)
            mix(0, 0, first=True)
            with pe.Fori(0, (B - 2) // 2) as i:
                mix(2 * i + 1, 1)
                mix(2 * i + 2, 0)
            mix(B - 1, 1, last=True)
            lora(B - 1, 1)
            lora_out(B - 1, 1)

            def proj(b, j, n):
                if n == 0:
                    pe.wait_ge(hc_ok, CREDIT + b + 1)
                    pe.wait_ge(cv_ok, CREDIT + b)
                elif n == 1:
                    pe.wait_ge(pq_ev, CREDIT + 4 * b)
                else:
                    pe.wait_ge(pq_ev, CREDIT + 4 * b + n - 1)
                if n < 4:
                    w = (wk1, wk1, wq1, wq1)[n]
                    last = nc.tensor.matmul(ps[:, n % 2, :], w[:, n % 2, :], h[:, j, :], start=True, stop=True)
                else:
                    pe.wait_ge(ctxs_in[j], 8 * (b - j) + 16)
                    for a in range(PATCH):
                        last = nc.tensor.matmul(ps[:, 0, a * E1:(a + 1) * E1], ctx_s[:, j, a * P:(a + 1) * P], wv1[:, :], start=True, stop=True)
                last.then_inc(pq_mm, 1)

            def scores(b, j, u):
                if u < 2:
                    pe.wait_ge(kb_ok, CREDIT + 2 * b + u + 1)
                    pe.wait_ge(pq_ev, CREDIT + 4 * b + 3 + u)
                pe.wait_ge(sb_ok, CREDIT + 8 * b + u - 1)
                nc.tensor.matmul(ps[:, 2 + u % 2, :], q_pad[:, j, u % 2, (u // 2) * P:(u // 2 + 1) * P],
                                 k_blk[:, j, u % 2, u // 2, :, :], start=True, stop=True).then_inc(s2_mm, 1)

            def turn(b, u):
                pe.wait_ge(p_ok, CREDIT + 8 * b + u + 1)
                pe.wait_ge(pt_ok, CREDIT + 8 * b + u - 1)
                for n in range(4):
                    last = nc.tensor.transpose(ps[:, 4 + u % 2, n * P:(n + 1) * P], p_w[:, u % 2, n * P:(n + 1) * P], ident[:, :])
                last.then_inc(pt_mm, 1)

            def weighted(b, j, u):
                patch, grp = divmod(u, 2)
                if u == 0:
                    pe.wait_ge(cv_ok, CREDIT + b + 1)
                    pe.wait_ge(ot_ev, CREDIT + b - 1)
                pe.wait_ge(pt_ok, CREDIT + 8 * b + u + 1)
                for n in range(4):
                    head = 4 * grp + n
                    at = (patch * H1 + head) * VA
                    last = nc.tensor.matmul(ps[:, 6 + j, at:at + VA], p_t[:, u % 2, n * P:(n + 1) * P], v_aug[:, j, patch, head, :],
                                            start=True, stop=True)
                last.then_inc(pv2_mm, 1)

            def turn_out(b, j):
                pe.wait_ge(on_ok, CREDIT + b + 1)
                for a in range(PATCH):
                    last = nc.tensor.matmul(ps[0:E1, 6 + j, a * P:(a + 1) * P], o_n[:, j, a * E1:(a + 1) * E1], ident[:, :],
                                            start=True, stop=True)
                last.then_inc(ot_mm, 1)

            def batch(b, j, first=False, last=False):
                for u in range(H1):
                    if u + 2 < H1:
                        scores(b, j, u + 2)
                    elif not last:
                        scores(b + 1, 1 - j, u + 2 - H1)
                    if not last and 1 <= u <= 5:
                        proj(b + 1, 1 - j, u - 1)
                    if u >= 1:
                        turn(b, u - 1)
                    elif not first:
                        turn(b - 1, H1 - 1)
                    if u >= 2:
                        weighted(b, j, u - 2)
                    elif not first:
                        weighted(b - 1, 1 - j, H1 - 2 + u)
                    if u == 4 and not first:
                        turn_out(b - 1, 1 - j)

            for n in range(5):
                proj(0, 0, n)
            scores(0, 0, 0)
            scores(0, 0, 1)
            batch(0, 0, first=True)
            with pe.Fori(0, (B - 2) // 2) as i:
                batch(2 * i + 1, 1)
                batch(2 * i + 2, 0)
            batch(B - 1, 1, last=True)
            turn(B - 1, H1 - 1)
            weighted(B - 1, 1, H1 - 2)
            weighted(B - 1, 1, H1 - 1)
            turn_out(B - 1, 1)

            def output(b, j):
                pe.wait_ge(gelu_ok, CREDIT + b + 1)
                pe.wait_ge(tc_ok, CREDIT + b - 1)
                nc.tensor.matmul(ps[:, 2 + j, :], wo1g[:, :], o_t[:, b, :], start=True, stop=True).then_inc(c2_mm, 1)

            def row_tiles(b):
                return [(xt_hi[:, k, b * P:(b + 1) * P], xt_lo[:, k, b * P:(b + 1) * P]) for k in range(KT)]

            def gate(b):
                pe.wait_ge(htl_ok, CREDIT + 2 * B + b + 1)
                product(ps[:, 3, b * EX:(b + 1) * EX], [(*row_tiles(b)[k], wg_hi[:, k, :], wg_lo[:, k, :])
                                                        for k in range(KT)]).then_inc(gate_mm, 1)

            def expert(e, j, b):
                pe.wait_ge(td_ok, CREDIT + B * e + b - 3)
                product(ps[:, 4 + b % 4, :], [(*row_tiles(b)[k], we_hi[j][:, k, :], we_lo[j][:, k, :]) for k in range(KT)]).then_inc(y2_mm, 1)

            pe.wait_ge(wo1_ok, CREDIT + 2)
            for b in range(3):
                output(b, b % 2)
            for b in range(3, B + 2):
                if b < B:
                    output(b, b % 2)
                turn_rows(2, b - 3, (b - 3) % 2, (b - 3) % 2)
            turn_rows(2, B - 1, 1, 1)

            for b in range(B):
                gate(b)
            pe.wait_ge(wel_ok, CREDIT + 4)
            for b in range(B):
                expert(0, 0, b)
            with pe.Fori(0, EX // 2 - 1) as i:
                pe.wait_ge(wel_ok, CREDIT + 8 * i + 8)
                for b in range(B):
                    expert(2 * i + 1, 1, b)
                pe.wait_ge(wel_ok, CREDIT + 8 * i + 12)
                for b in range(B):
                    expert(2 * i + 2, 0, b)
            pe.wait_ge(wel_ok, CREDIT + 4 * EX)
            for b in range(B):
                expert(EX - 1, 1, b)


def _constants():
    import numpy as np

    inv_freq = np.float32(1.0) / np.float32(10000.0) ** (np.arange(0, P, 2, dtype=np.float32) / np.float32(P))
    phase = np.arange(P, dtype=np.float32)[None, :] * np.tile(inv_freq, 2)[:, None]
    sin = np.sin(phase)
    sin[P // 2:] *= -1.0
    aug = np.zeros((P, 3), np.float32)
    row = np.arange(P) % 32
    penalty = np.float32(1e9 * DH**0.5)
    aug[:, 0] = np.where(row == DH, penalty, 1.0)
    aug[:, 1] = np.where(row == DH, -penalty, 0.0)
    aug[:, 2] = row == DH
    lower = np.broadcast_to(np.tril(np.ones((EX, EX), np.float32), -1), (P, EX, EX))
    return {
        "ident": np.eye(P, dtype=np.float32), "cos": np.cos(phase).astype(np.float32), "sin": sin.astype(np.float32),
        "aug": aug, "iota": np.broadcast_to(np.arange(ET, dtype=np.float32), (P, ET)), "lower": lower,
    }


def kernel(x, ctx_4096, mask_1x1xSxS2_bk0, mask_Bx1x4096_ff1, g_xattn, g_ffn, L0_xattn_Wq, L0_xattn_Wk, L0_xattn_Wv,
           L0_xattn_Wo, L0_ffn_W_base, L0_ffn_b_base, L0_ffn_lora_A, L0_ffn_lora_B, L0_ffn_router_W, L0_ffn_router_b,
           L0_ffn_domain_prior, L0_ffn_active, L1_xattn_Wq, L1_xattn_bq, L1_xattn_Wk, L1_xattn_bk, L1_xattn_Wv,
           L1_xattn_bv, L1_xattn_Wo, L1_xattn_bo, L1_ffn_W_gate, L1_ffn_b_gate, L1_ffn_W_e, L1_ffn_b_e):
    import concourse.bacc as bacc
    import numpy as np
    from concourse.bass_utils import run_bass_kernel_spmd

    def pad_heads(w):
        w = np.asarray(w)
        wide = np.zeros(w.shape[:-1] + (2, 4, 32), w.dtype)
        wide[..., :DH] = w.reshape(w.shape[:-1] + (2, 4, DH))
        return wide.reshape(w.shape[:-1] + (2, P))

    c = _constants()
    arrays = [
        ("x", x), ("ctx", ctx_4096), ("ctx_t", np.asarray(ctx_4096).reshape(N, D).T),
        ("mask_tq", np.asarray(mask_1x1xSxS2_bk0)[0, 0].T), ("mask_b", mask_Bx1x4096_ff1),
        ("g_xattn", g_xattn), ("g_ffn", g_ffn), ("wq0", L0_xattn_Wq), ("wk0", L0_xattn_Wk), ("wv0", L0_xattn_Wv),
        ("wo0", L0_xattn_Wo), ("wbase_t", np.asarray(L0_ffn_W_base).T), ("bbase", L0_ffn_b_base),
        ("lora_a_t", np.asarray(L0_ffn_lora_A).reshape(ET * RANK, D).T),
        ("lora_b", np.asarray(L0_ffn_lora_B).transpose(0, 2, 1).reshape(ET * RANK, D)),
        ("router_t", np.asarray(L0_ffn_router_W).T), ("router_b", L0_ffn_router_b), ("prior", L0_ffn_domain_prior),
        ("active", L0_ffn_active),
        ("wq1p", pad_heads(np.asarray(L1_xattn_Wq).T)), ("bq1p", pad_heads(L1_xattn_bq).T),
        ("wk1p", pad_heads(np.asarray(L1_xattn_Wk).T)), ("bk1p", pad_heads(L1_xattn_bk).T),
        ("wv1t", np.asarray(L1_xattn_Wv).T), ("bv1", L1_xattn_bv), ("wo1t", np.asarray(L1_xattn_Wo).T), ("bo1", L1_xattn_bo),
        ("wgate", L1_ffn_W_gate), ("bgate", L1_ffn_b_gate), ("we", L1_ffn_W_e), ("be", L1_ffn_b_e),
        ("c_ident", c["ident"]), ("c_cos", c["cos"]), ("c_sin", c["sin"]), ("c_aug", c["aug"]), ("c_iota", c["iota"]),
        ("c_lower", c["lower"]),
    ]
    nc = bacc.Bacc("TRN2", target_bir_lowering=False, num_devices=1)
    feed, args = {}, []
    for name, a in arrays:
        a = np.ascontiguousarray(a)
        feed["in_" + name] = a
        args.append(nc.dram_tensor("in_" + name, a.shape, mybir.dt.from_np(a.dtype), kind="ExternalInput").ap())
    args.append(nc.dram_tensor("out_x", (B, P, D), F32, kind="ExternalOutput").ap())
    flamingo_gated_two_layers(nc, *args)
    return run_bass_kernel_spmd(nc, [feed], core_ids=[0]).results[0]["out_x"]
```
